# Optimizing a Trainium2 kernel written in Bass

```python
import numpy as np
import jax
import jax.numpy as jnp

def _softmax(x, axis=-1):
    return jax.nn.softmax(x, axis=axis)

def _gelu(x):
    return jax.nn.gelu(x, approximate=True)

def _silu(x):
    return jax.nn.silu(x)

def _sigmoid(x):
    return jax.nn.sigmoid(x)

def _layernorm(x, axis=-1, eps=1e-05):
    m = jnp.mean(x, axis=axis, keepdims=True)
    v = jnp.var(x, axis=axis, keepdims=True)
    return (x - m) / jnp.sqrt(v + eps)

def _scatter_add(tgt, idx, src, axis=0):
    return tgt.at[idx].add(src)

def _segment_sum(src, seg, n):
    return jax.ops.segment_sum(src, seg, n)
kernel_name = 'mk_lm_tower_d1_tok_ids1024_r4_3a158e'

def setup_inputs(seed: int=0):
    np.random.seed(seed)
    _w = jnp.asarray

    def _rec_inputs():
        import jax
        import jax.numpy as jnp
        _rk = jax.random.key(seed)
        x = jax.random.randint(jax.random.fold_in(_rk, 1), (8, 256), 0, 12564, jnp.int32)
        return x
    x = _rec_inputs()

    def _L0_tok_setup():
        import jax, jax.numpy as jnp
        import numpy as np
        V, D = (50257, 256)
        B, S = (8, 512)
        DROPOUT = 0.1
        key = jax.random.key(seed)
        k1, k2, k3 = jax.random.split(key, 3)
        input_ids = jax.random.randint(k1, (B, S), 0, V, dtype=jnp.int64)
        weight = jax.random.normal(k2, (V, D), dtype=jnp.float32)
        mask_u = jax.random.uniform(k3, (V, D), dtype=jnp.float32)
        return {'input_ids': input_ids, 'weight': weight, 'mask_u': mask_u}
    _L0_tok_all = _L0_tok_setup()
    _L0_tok_in = {k: v for k, v in _L0_tok_all.items() if k in ('weight', 'mask_u')}
    del _L0_tok_all

    def _L0_attn_setup():
        import jax, jax.numpy as jnp
        import numpy as np
        D_MODEL = 256
        N_HEADS = 16
        D_HEAD = 64
        ROTARY_DIM = 64
        ROTARY_BASE = 10000.0
        ATTN_SCALE = 8.0

        def _rope_sin_cos(n_pos, rotary_dim):
            pos = jnp.arange(n_pos, dtype=jnp.float32)
            dim = jnp.arange(rotary_dim // 2, dtype=jnp.float32)
            freq = ROTARY_BASE ** (dim / (rotary_dim / 2))
            freq = jnp.concatenate([freq, freq])
            angles = pos[:, None] / freq[None, :]
            return (jnp.sin(angles), jnp.cos(angles))

        def _apply_rotary(x, sin, cos):
            n = x.shape[-1] // 2
            x_flip = jnp.concatenate([-x[..., n:], x[..., :n]], axis=-1)
            return x * cos[None, :, None, :] + x_flip * sin[None, :, None, :]
        key = jax.random.key(seed)
        ks = jax.random.split(key, 9)
        std = 0.02
        x = jax.random.normal(ks[0], (2, 512, D_MODEL), dtype=jnp.float32)
        W_Q = jax.random.normal(ks[1], (N_HEADS, D_MODEL, D_HEAD), dtype=jnp.float32) * std
        W_K = jax.random.normal(ks[2], (N_HEADS, D_MODEL, D_HEAD), dtype=jnp.float32) * std
        W_V = jax.random.normal(ks[3], (N_HEADS, D_MODEL, D_HEAD), dtype=jnp.float32) * std
        W_O = jax.random.normal(ks[4], (N_HEADS, D_HEAD, D_MODEL), dtype=jnp.float32) * std
        b_Q = jnp.zeros((N_HEADS, D_HEAD), dtype=jnp.float32)
        b_K = jnp.zeros((N_HEADS, D_HEAD), dtype=jnp.float32)
        b_V = jnp.zeros((N_HEADS, D_HEAD), dtype=jnp.float32)
        b_O = jnp.zeros((D_MODEL,), dtype=jnp.float32)
        return {'x': x, 'W_Q': W_Q, 'b_Q': b_Q, 'W_K': W_K, 'b_K': b_K, 'W_V': W_V, 'b_V': b_V, 'W_O': W_O, 'b_O': b_O}
    _L0_attn_all = _L0_attn_setup()
    _L0_attn_in = {k: v for k, v in _L0_attn_all.items() if k in ('W_Q', 'b_Q', 'W_K', 'b_K', 'W_V', 'b_V', 'W_O', 'b_O')}
    del _L0_attn_all

    def _L0_ffn_setup():
        import jax, jax.numpy as jnp
        import numpy as np
        DIM = 256
        DEPTH = 6
        HEADS = 16
        DIM_HEAD = 64
        WINDOW = 64
        INNER = HEADS * DIM_HEAD
        DIM_INNER = int(DIM * 4 * 2 / 3)
        QK_SCALE = 8.0

        def shift_tokens(t):
            a, s = jnp.split(t, 2, -1)
            s = jnp.pad(s, ((0, 0), (1, 0), (0, 0)))[:, :-1]
            return jnp.concatenate([a, s], -1)

        def l2norm(t):
            return t / jnp.maximum(jnp.linalg.norm(t, axis=-1, keepdims=True), 1e-12)

        def rotate_half(x):
            x1, x2 = jnp.split(x, 2, -1)
            return jnp.concatenate([-x2, x1], -1)

        def rotary_tables(n):
            half = jnp.arange(0, DIM_HEAD, 2, dtype=jnp.float32)
            inv_freq = 1.0 / 10000.0 ** (half / DIM_HEAD)
            t = jnp.arange(n, dtype=jnp.float32)
            freqs = t[:, None] * inv_freq[None, :]
            freqs = jnp.concatenate([freqs, freqs], -1)
            base_scale = (half + 0.4 * DIM_HEAD) / (1.4 * DIM_HEAD)
            power = (t - n // 2) / (WINDOW // 2)
            scale = base_scale[None, :] ** power[:, None]
            scale = jnp.concatenate([scale, scale], -1)
            return (freqs, scale)

        def local_attention(q, k, v):
            b, h, n, d = q.shape
            w = WINDOW
            nw = n // w
            bq = q.reshape(b, h, nw, w, d)
            bk = k.reshape(b, h, nw, w, d)
            bv = v.reshape(b, h, nw, w, d)

            def look(t):
                p = jnp.pad(t, ((0, 0), (0, 0), (1, 0), (0, 0), (0, 0)))
                return jnp.concatenate([p[:, :, :nw], p[:, :, 1:]], axis=3)
            bk2, bv2 = (look(bk), look(bv))
            seq = jnp.arange(n).reshape(nw, w)
            seq_p = jnp.pad(seq, ((1, 0), (0, 0)), constant_values=-1)
            jt = jnp.concatenate([seq_p[:nw], seq_p[1:]], axis=1)
            it = seq[:, :, None]
            jb = jt[:, None, :]
            mask = (it < jb) | (it > jb + w) | (jb == -1)
            sim = jnp.einsum('bhwie,bhwje->bhwij', bq, bk2) * QK_SCALE
            sim = jnp.where(mask, -jnp.finfo(sim.dtype).max, sim)
            attn = jax.nn.softmax(sim, -1)
            out = jnp.einsum('bhwij,bhwje->bhwie', attn, bv2)
            return out.reshape(b, h, n, d)

        def attn_layer(x, Wqkv, qs, ksc, Wo):
            b, n, _ = x.shape
            qkv = x @ Wqkv
            q, k, v = jnp.split(qkv, 3, -1)
            sh = lambda t: t.reshape(b, n, HEADS, DIM_HEAD).transpose(0, 2, 1, 3)
            q, k, v = (sh(q), sh(k), sh(v))
            q = l2norm(q) * qs
            k = l2norm(k) * ksc
            freqs, scale = rotary_tables(n)
            cos, sin = (jnp.cos(freqs), jnp.sin(freqs))
            q = q * cos * scale + rotate_half(q) * sin * scale
            inv = 1.0 / scale
            k = k * cos * inv + rotate_half(k) * sin * inv
            out = local_attention(q, k, v)
            out = out.transpose(0, 2, 1, 3).reshape(b, n, INNER)
            return out @ Wo

        def ffn_layer(x, g, bln, W1, b1, W2, b2):
            mu = x.mean(-1, keepdims=True)
            var = ((x - mu) ** 2).mean(-1, keepdims=True)
            xn = (x - mu) / jnp.sqrt(var + 1e-05) * g + bln
            hg = xn @ W1 + b1
            a, gate = jnp.split(hg, 2, -1)
            return a * jax.nn.gelu(gate, approximate=False) @ W2 + b2
        key = jax.random.key(seed)
        ks = jax.random.split(key, 8)
        B, N = (2, 512)
        init = lambda k, shape: jax.random.normal(k, shape, jnp.float32) * 0.02
        return {'x': jax.random.normal(ks[0], (B, N, DIM), jnp.float32), 'Wqkv': init(ks[1], (DEPTH, DIM, 3 * INNER)), 'q_scale': jnp.ones((DEPTH, DIM_HEAD), jnp.float32), 'k_scale': jnp.ones((DEPTH, DIM_HEAD), jnp.float32), 'Wo': init(ks[2], (DEPTH, INNER, DIM)), 'ln_g': jnp.ones((DEPTH, DIM), jnp.float32), 'ln_b': jnp.zeros((DEPTH, DIM), jnp.float32), 'W1': init(ks[3], (DEPTH, DIM, 2 * DIM_INNER)), 'b1': jnp.zeros((DEPTH, 2 * DIM_INNER), jnp.float32), 'W2': init(ks[4], (DEPTH, DIM_INNER, DIM)), 'b2': jnp.zeros((DEPTH, DIM), jnp.float32)}
    _L0_ffn_all = _L0_ffn_setup()
    _L0_ffn_in = {k: v for k, v in _L0_ffn_all.items() if k in ('Wqkv', 'q_scale', 'k_scale', 'Wo', 'ln_g', 'ln_b', 'W1', 'b1', 'W2', 'b2')}
    del _L0_ffn_all
    return {'x': x, 'L0_tok_weight': _L0_tok_in['weight'], 'L0_tok_mask_u': _L0_tok_in['mask_u'], 'L0_attn_W_Q': _L0_attn_in['W_Q'], 'L0_attn_b_Q': _L0_attn_in['b_Q'], 'L0_attn_W_K': _L0_attn_in['W_K'], 'L0_attn_b_K': _L0_attn_in['b_K'], 'L0_attn_W_V': _L0_attn_in['W_V'], 'L0_attn_b_V': _L0_attn_in['b_V'], 'L0_attn_W_O': _L0_attn_in['W_O'], 'L0_attn_b_O': _L0_attn_in['b_O'], 'L0_ffn_Wqkv': _L0_ffn_in['Wqkv'], 'L0_ffn_q_scale': _L0_ffn_in['q_scale'], 'L0_ffn_k_scale': _L0_ffn_in['k_scale'], 'L0_ffn_Wo': _L0_ffn_in['Wo'], 'L0_ffn_ln_g': _L0_ffn_in['ln_g'], 'L0_ffn_ln_b': _L0_ffn_in['ln_b'], 'L0_ffn_W1': _L0_ffn_in['W1'], 'L0_ffn_b1': _L0_ffn_in['b1'], 'L0_ffn_W2': _L0_ffn_in['W2'], 'L0_ffn_b2': _L0_ffn_in['b2']}

def reference(x, L0_tok_weight, L0_tok_mask_u, L0_attn_W_Q, L0_attn_b_Q, L0_attn_W_K, L0_attn_b_K, L0_attn_W_V, L0_attn_b_V, L0_attn_W_O, L0_attn_b_O, L0_ffn_Wqkv, L0_ffn_q_scale, L0_ffn_k_scale, L0_ffn_Wo, L0_ffn_ln_g, L0_ffn_ln_b, L0_ffn_W1, L0_ffn_b1, L0_ffn_W2, L0_ffn_b2):
    import jax
    import jax.numpy as jnp

    def _L0_tok_ref(input_ids, weight, mask_u):
        import jax, jax.numpy as jnp
        import numpy as np
        V, D = (50257, 256)
        B, S = (8, 512)
        DROPOUT = 0.1
        keep = 1.0 - DROPOUT
        mask = (mask_u < keep).astype(weight.dtype) / keep
        masked_weight = weight * mask
        return jnp.take(masked_weight, input_ids, axis=0)

    def _L0_attn_ref(x, W_Q, b_Q, W_K, b_K, W_V, b_V, W_O, b_O):
        import jax, jax.numpy as jnp
        import numpy as np
        D_MODEL = 256
        N_HEADS = 16
        D_HEAD = 64
        ROTARY_DIM = 64
        ROTARY_BASE = 10000.0
        ATTN_SCALE = 8.0

        def _rope_sin_cos(n_pos, rotary_dim):
            pos = jnp.arange(n_pos, dtype=jnp.float32)
            dim = jnp.arange(rotary_dim // 2, dtype=jnp.float32)
            freq = ROTARY_BASE ** (dim / (rotary_dim / 2))
            freq = jnp.concatenate([freq, freq])
            angles = pos[:, None] / freq[None, :]
            return (jnp.sin(angles), jnp.cos(angles))

        def _apply_rotary(x, sin, cos):
            n = x.shape[-1] // 2
            x_flip = jnp.concatenate([-x[..., n:], x[..., :n]], axis=-1)
            return x * cos[None, :, None, :] + x_flip * sin[None, :, None, :]
        B, S, _ = x.shape
        q = jnp.einsum('bsd,hdk->bshk', x, W_Q) + b_Q
        k = jnp.einsum('bsd,hdk->bshk', x, W_K) + b_K
        v = jnp.einsum('bsd,hdk->bshk', x, W_V) + b_V
        sin, cos = _rope_sin_cos(S, ROTARY_DIM)
        q = _apply_rotary(q, sin, cos)
        k = _apply_rotary(k, sin, cos)
        scores = jnp.einsum('bqhd,bkhd->bhqk', q, k) / ATTN_SCALE
        causal = jnp.tril(jnp.ones((S, S), dtype=bool))
        scores = jnp.where(causal[None, None], scores, -jnp.inf)
        pattern = jax.nn.softmax(scores, axis=-1)
        pattern = jnp.where(jnp.isnan(pattern), jnp.zeros_like(pattern), pattern)
        z = jnp.einsum('bhqk,bkhd->bqhd', pattern, v)
        out = jnp.einsum('bqhd,hdm->bqm', z, W_O) + b_O
        return out

    def _L0_ffn_ref(x, Wqkv, q_scale, k_scale, Wo, ln_g, ln_b, W1, b1, W2, b2):
        import jax, jax.numpy as jnp
        import numpy as np
        DIM = 256
        DEPTH = 6
        HEADS = 16
        DIM_HEAD = 64
        WINDOW = 64
        INNER = HEADS * DIM_HEAD
        DIM_INNER = int(DIM * 4 * 2 / 3)
        QK_SCALE = 8.0

        def shift_tokens(t):
            a, s = jnp.split(t, 2, -1)
            s = jnp.pad(s, ((0, 0), (1, 0), (0, 0)))[:, :-1]
            return jnp.concatenate([a, s], -1)

        def l2norm(t):
            return t / jnp.maximum(jnp.linalg.norm(t, axis=-1, keepdims=True), 1e-12)

        def rotate_half(x):
            x1, x2 = jnp.split(x, 2, -1)
            return jnp.concatenate([-x2, x1], -1)

        def rotary_tables(n):
            half = jnp.arange(0, DIM_HEAD, 2, dtype=jnp.float32)
            inv_freq = 1.0 / 10000.0 ** (half / DIM_HEAD)
            t = jnp.arange(n, dtype=jnp.float32)
            freqs = t[:, None] * inv_freq[None, :]
            freqs = jnp.concatenate([freqs, freqs], -1)
            base_scale = (half + 0.4 * DIM_HEAD) / (1.4 * DIM_HEAD)
            power = (t - n // 2) / (WINDOW // 2)
            scale = base_scale[None, :] ** power[:, None]
            scale = jnp.concatenate([scale, scale], -1)
            return (freqs, scale)

        def local_attention(q, k, v):
            b, h, n, d = q.shape
            w = WINDOW
            nw = n // w
            bq = q.reshape(b, h, nw, w, d)
            bk = k.reshape(b, h, nw, w, d)
            bv = v.reshape(b, h, nw, w, d)

            def look(t):
                p = jnp.pad(t, ((0, 0), (0, 0), (1, 0), (0, 0), (0, 0)))
                return jnp.concatenate([p[:, :, :nw], p[:, :, 1:]], axis=3)
            bk2, bv2 = (look(bk), look(bv))
            seq = jnp.arange(n).reshape(nw, w)
            seq_p = jnp.pad(seq, ((1, 0), (0, 0)), constant_values=-1)
            jt = jnp.concatenate([seq_p[:nw], seq_p[1:]], axis=1)
            it = seq[:, :, None]
            jb = jt[:, None, :]
            mask = (it < jb) | (it > jb + w) | (jb == -1)
            sim = jnp.einsum('bhwie,bhwje->bhwij', bq, bk2) * QK_SCALE
            sim = jnp.where(mask, -jnp.finfo(sim.dtype).max, sim)
            attn = jax.nn.softmax(sim, -1)
            out = jnp.einsum('bhwij,bhwje->bhwie', attn, bv2)
            return out.reshape(b, h, n, d)

        def attn_layer(x, Wqkv, qs, ksc, Wo):
            b, n, _ = x.shape
            qkv = x @ Wqkv
            q, k, v = jnp.split(qkv, 3, -1)
            sh = lambda t: t.reshape(b, n, HEADS, DIM_HEAD).transpose(0, 2, 1, 3)
            q, k, v = (sh(q), sh(k), sh(v))
            q = l2norm(q) * qs
            k = l2norm(k) * ksc
            freqs, scale = rotary_tables(n)
            cos, sin = (jnp.cos(freqs), jnp.sin(freqs))
            q = q * cos * scale + rotate_half(q) * sin * scale
            inv = 1.0 / scale
            k = k * cos * inv + rotate_half(k) * sin * inv
            out = local_attention(q, k, v)
            out = out.transpose(0, 2, 1, 3).reshape(b, n, INNER)
            return out @ Wo

        def ffn_layer(x, g, bln, W1, b1, W2, b2):
            mu = x.mean(-1, keepdims=True)
            var = ((x - mu) ** 2).mean(-1, keepdims=True)
            xn = (x - mu) / jnp.sqrt(var + 1e-05) * g + bln
            hg = xn @ W1 + b1
            a, gate = jnp.split(hg, 2, -1)
            return a * jax.nn.gelu(gate, approximate=False) @ W2 + b2
        for i in range(DEPTH):
            x = attn_layer(shift_tokens(x), Wqkv[i], q_scale[i], k_scale[i], Wo[i]) + x
            x = ffn_layer(shift_tokens(x), ln_g[i], ln_b[i], W1[i], b1[i], W2[i], b2[i]) + x
        return x
    h = _L0_tok_ref(x, L0_tok_weight, L0_tok_mask_u)
    h = h + _L0_attn_ref(_layernorm(h, axis=-1), L0_attn_W_Q, L0_attn_b_Q, L0_attn_W_K, L0_attn_b_K, L0_attn_W_V, L0_attn_b_V, L0_attn_W_O, L0_attn_b_O)
    h = h + _L0_ffn_ref(_layernorm(h, axis=-1), L0_ffn_Wqkv, L0_ffn_q_scale, L0_ffn_k_scale, L0_ffn_Wo, L0_ffn_ln_g, L0_ffn_ln_b, L0_ffn_W1, L0_ffn_b1, L0_ffn_W2, L0_ffn_b2)
    return h

_drawn_inputs = setup_inputs


def setup_inputs(seed=0):
    import zlib

    import numpy as np

    out = dict(_drawn_inputs(seed))
    spreads = {'L0_attn_b_Q': (0.0, 0.8),
     'L0_attn_b_K': (0.0, 0.8),
     'L0_attn_b_V': (0.0, 0.1),
     'L0_attn_b_O': (0.0, 0.1),
     'L0_ffn_q_scale': (1.0, 0.6),
     'L0_ffn_k_scale': (1.0, 0.6),
     'L0_ffn_ln_g': (1.0, 0.6),
     'L0_ffn_ln_b': (0.0, 0.8),
     'L0_ffn_b1': (0.0, 0.471),
     'L0_ffn_b2': (0.0, 0.1)}
    factors = {'L0_attn_W_Q': 8.0, 'L0_attn_W_K': 8.0}
    for name, (base, spread) in spreads.items():
        noise = np.random.default_rng([zlib.crc32(name.encode()), seed]).standard_normal(out[name].shape)
        drawn = base * np.exp(spread * noise) if base else spread * noise
        out[name] = jnp.asarray(drawn.astype(out[name].dtype))
    for name, factor in factors.items():
        out[name] = (out[name] * factor).astype(out[name].dtype)
    return out
```

```python
from collections import namedtuple
from contextlib import ExitStack

import numpy as np
import concourse.bass as bass
from concourse import mybir
from concourse.alu_op_type import AluOpType as ALU

SEQS, SEQ, DIM = 8, 256, 256
HEADS, DH = 16, 64
DEPTH, WINDOW = 6, 64
INNER = HEADS * DH
HID = 682
P = 128
KD = DIM // P
TT = SEQ // P
HALF = INNER // 2
UNITS = 4
PAIRS = HEADS // 2
MT = -(-HID // P)
MLAST = HID - (MT - 1) * P
KEEP = 1.0 - 0.1

CHUNKS = [(kind, t, half) for half in range(2) for kind in range(3) for t in range(TT)]
NCH = len(CHUNKS)
QK_SLOT = [c for c, (kind, _, _) in enumerate(CHUNKS) if kind < 2]

UP_BANK = (0, 1, 0, 1, 1, 0)

N_NEWTON = 11
N_LN = 3 + N_NEWTON

Stage = namedtuple("Stage", "kind seq layer")
Body = namedtuple("Body", "q a f n_q n_a n_f n_ln")


def constants():
    f32 = np.float32
    half = np.arange(0, DH, 2, dtype=f32)
    pos = np.arange(SEQ, dtype=f32)

    def tables(angle, scale_q, scale_k, gain):
        cos, sin = np.cos(angle), np.sin(angle)
        sgn = np.where(np.arange(DH) < DH // 2, -1, 1).astype(f32)
        return np.stack([cos * scale_q * gain, sin * sgn * scale_q * gain,
                         cos * scale_k, sin * sgn * scale_k], 1).astype(f32)

    dim = np.arange(DH // 2, dtype=f32)
    freq = (f32(10000.0) ** (dim / f32(DH / 2))).astype(f32)
    freq = np.concatenate([freq, freq])
    tab_g = tables((pos[:, None] / freq[None]).astype(f32), 1, 1, 1 / 8)
    inv = (1.0 / f32(10000.0) ** (half / f32(DH))).astype(f32)
    ang = (pos[:, None] * inv[None]).astype(f32)
    ang = np.concatenate([ang, ang], -1)
    base = ((half + 0.4 * DH) / (1.4 * DH)).astype(f32)
    power = ((pos - SEQ // 2) / (WINDOW // 2)).astype(f32)
    scale = (base[None] ** power[:, None]).astype(f32)
    scale = np.concatenate([scale, scale], -1)
    tab_l = tables(ang, scale, (1 / scale).astype(f32), 8)

    def tiled(t):
        return np.ascontiguousarray(t.reshape(TT, P, 4, DH).transpose(1, 0, 2, 3))

    i, j = np.arange(SEQ)[:, None], np.arange(SEQ)[None]
    neg = f32(-1e30)
    causal = np.where(j <= i, f32(0), neg)
    local = np.where((j <= i) & (i <= j + WINDOW), f32(0), neg)
    bf16 = mybir.dt.np(mybir.dt.bfloat16)
    masks = np.concatenate([causal[:P, :P], causal[P:, :], local[:P, :P], local[P:, WINDOW:]], 1)
    return {"tab_g": tiled(tab_g), "tab_l": tiled(tab_l), "masks": masks.astype(bf16),
            "eye16": np.eye(P, dtype=f32).astype(bf16), "eye32": np.eye(P, dtype=f32)}


def tower_kernel(nc, ids, emb_w, emb_u, wq, wk, wv, bqkv, wo, bo, l_wqkv, l_qk_scale, l_wo, l_par,
                 l_w1, l_w2, tab_g, tab_l, masks, eye16, eye32, out):
    f32, bf16, i32 = mybir.dt.float32, mybir.dt.bfloat16, mybir.dt.int32
    ACT = mybir.ActivationFunctionType
    AX = mybir.AxisListType
    ds = bass.ds

    ctx = ExitStack()
    with ctx:
        def sb(name, shape, dt=f32):
            return ctx.enter_context(nc.sbuf_tensor(name, shape, dt))

        def pb(name):
            return ctx.enter_context(nc.psum_tensor(name, [P, 512], f32))

        def sem(name):
            return ctx.enter_context(nc.semaphore(name))

        hT = sb("hT", [P, KD, SEQS, SEQ])
        xT = sb("xT", [P, KD, SEQS, SEQ + 1])
        Wqkv = sb("Wqkv", [P, KD, 3, INNER])
        Wo = sb("Wo", [P, PAIRS, DIM])
        WF = sb("WF", [P, KD * 2 * HID + MT * DIM])
        W1 = WF[:, 0:KD * 2 * HID].rearrange("p (k n) -> p k n", k=KD)
        W2 = WF[:, KD * 2 * HID:].rearrange("p (m n) -> p m n", m=MT)
        tabG = sb("tabG", [P, TT, 4, DH])
        tabB = sb("tabB", [P, TT, 4, DH])
        tabL = sb("tabL", [P, TT, 4, DH])
        qks = sb("qks", [P, DEPTH, 2, DH])
        par = sb("par", [P, DEPTH, 18])
        bO = sb("bO", [P, KD])
        bQKV = sb("bQKV", [1, 3, INNER])
        ones1 = sb("ones1", [1, P])
        onesN = sb("onesN", [P, P])
        idb = sb("idb", [P, P], bf16)
        idf = sb("idf", [P, P])
        mk = sb("mk", [P, P + SEQ + P + SEQ - WINDOW], bf16)
        idx = sb("idx", [P, SEQS * TT], i32)
        xs = sb("xs", [P, KD, SEQ])
        raw = sb("raw", [P, 2, HALF])
        sq = sb("sq", [P, 2, HALF])
        t2 = sb("t2", [P, 2, HALF])
        qr = sb("qr", [P, TT, 2, INNER])
        ssq = sb("ssq", [P, 4 * 8])
        rn = sb("rn", [P, 4 * 8])
        nt = sb("nt", [P, 4 * 8])
        V = sb("V", [P, TT, INNER])
        qT = sb("qT", [P, 2, 2, SEQ])
        kT = sb("kT", [P, 2, 2, 2, SEQ])
        Pr = sb("Pr", [P, TT, 4, SEQ])
        nm = sb("nm", [P, 2, 8])
        rs = sb("rs", [P, 2, 8])
        rr = sb("rr", [P, 2, 8])
        PT = sb("PT", [P, 4, P + SEQ])
        OT = sb("OT", [P, PAIRS, SEQ])
        xf = sb("xf", [P, KD, SEQ])
        xc = sb("xc", [P, KD, SEQ])
        sqF = sb("sqF", [P, KD, SEQ])
        vr = sb("vr", [P, SEQ])
        ry = sb("ry", [P, SEQ])
        rt = sb("rt", [P, SEQ])
        bG = sb("bG", [P, MT])
        xn = sb("xn", [P, KD, SEQ])
        G = sb("G", [P, MT, SEQ])
        gw = qr[:, :, :, :].rearrange("p a b (c d) -> p (a b c) d", d=DIM)
        gu = WF[:, 0:SEQS * TT * DIM].rearrange("p (t c) -> p t c", c=DIM)
        em = V[:, 0, 0:TT * DIM].rearrange("p (t c) -> p t c", c=DIM)
        yb, yo = xf, xc

        A = [pb("A0"), pb("A1")]
        T = [pb("T0"), pb("T1")]
        S0 = pb("S0")
        S1 = ctx.enter_context(nc.psum_tensor("S1", [P, 2, 512], f32))
        O = pb("O")

        s_const, s_ids, s_gat, s_out = sem("const"), sem("ids"), sem("gather"), sem("out")
        w_q = [sem(f"w_q{j}") for j in range(6)]
        w_o, w_1, w_2 = sem("w_o"), sem("w_1"), sem("w_2")
        zeroed, pad_ready = sem("zeroed"), sem("pad_ready")
        pe_e, pe_y = sem("pe_e"), sem("pe_y")
        pe_q, pe_tq, pe_tk = sem("pe_q"), sem("pe_tq"), sem("pe_tk")
        pe_s0, pe_s1, pe_pt, pe_o, pe_wo = (sem(x) for x in ("pe_s0", "pe_s1", "pe_pt", "pe_o", "pe_wo"))
        pe_ln, pe_w1, pe_w2 = sem("pe_ln"), sem("pe_w1"), sem("pe_w2")
        a_e, a_y = sem("a_e"), sem("a_y")
        a_q, a_qT, a_x0, a_x1, a_pt, a_sq, a_gelu = (sem(x) for x in ("a_q", "a_qT", "a_x0", "a_x1", "a_pt", "a_sq", "a_gelu"))
        v_em, v_y = sem("v_em"), sem("v_y")
        v_xs, v_kT, v_max, v_rec = sem("v_xs"), sem("v_kT"), sem("v_max"), sem("v_rec")
        v_rot, v_rn, v_ot, v_res = sem("v_rot"), sem("v_rn"), sem("v_ot"), sem("v_res")
        v_xf, v_ln, v_xn, v_hid, v_out = sem("v_xf"), sem("v_ln"), sem("v_xn"), sem("v_hid"), sem("v_out")
        v_nrm, v_tab, v_emb, v_bG = sem("v_nrm"), sem("v_tab"), sem("v_emb"), sem("v_bG")
        g_add, g_rot, g_p = sem("g_add"), sem("g_rot"), sem("g_p")

        block = ctx.enter_context(nc.Block())

        def least(value):
            return max(value, 0) if isinstance(value, int) else value

        def bodies(eng, body):
            def g(q, a, f):
                body(Body(Stage("G", q, 0), None if a is None else Stage("G", a, 0),
                          None if f is None else Stage("G", f, 0),
                          q, 0 if a is None else a, 0, SEQS + (0 if f is None else f)))

            def l(layer, s, before="L"):
                n = SEQS * layer + s
                prev = "L" if before == "L" else "G"
                if isinstance(s, int) and s == 0:
                    a, f = Stage(prev, SEQS - 1, layer - 1), Stage(prev, SEQS - 2, layer - 1)
                elif isinstance(s, int) and s == 1:
                    a, f = Stage("L", 0, layer), Stage(prev, SEQS - 1, layer - 1)
                else:
                    a, f = Stage("L", s - 1, layer), Stage("L", s - 2, layer)
                n_f = 0 if f.kind == "G" else n - 2
                body(Body(Stage("L", s, layer), a, f, SEQS + n, SEQS + n - 1, n_f, 2 * SEQS + n - 2))

            g(0, None, None)
            g(1, 0, None)
            with eng.Fori(2, SEQS) as s:
                g(s, s - 1, s - 2)
            l(0, 0, "G")
            l(0, 1, "G")
            l(0, 2)
            with eng.Fori(3, SEQS) as s:
                l(0, s)
            with eng.Fori(1, DEPTH) as layer:
                l(layer, 0)
                l(layer, 1)
                with eng.Fori(2, SEQS) as s:
                    l(layer, s)
            n = SEQS * DEPTH
            last = DEPTH - 1
            body(Body(None, Stage("L", SEQS - 1, last), Stage("L", SEQS - 2, last),
                      SEQS + n, SEQS + n - 1, n - 2, 2 * SEQS + n - 2))
            body(Body(None, None, Stage("L", SEQS - 1, last), SEQS + n, SEQS + n, n - 1, 2 * SEQS + n - 1))

        def sequences(eng, step):
            step(0)
            with eng.Fori(1, SEQS) as s:
                step(s)

        @block.sync
        def _(sp):
            sp.dma_start(idx[:, :], ids).then_inc(s_ids, 16)
            consts = [(tabG, tab_g), (tabB, tab_l), (idb, eye16), (idf, eye32), (mk, masks), (par, l_par), (bO, bo)]
            sp.dma_start(bQKV[:, :, :], bqkv).then_inc(s_const, 16)
            for dst, src in consts:
                sp.dma_start(dst[:], src).then_inc(s_const, 16)
            sp.dma_start(qks[:].rearrange("p l k d -> p (l k d)"), l_qk_scale.to_broadcast((P, DEPTH * 2 * DH))).then_inc(s_const, 16)

            def load_wo(src):
                sp.dma_start(Wo[:, :, :], src.rearrange("(a p) m -> p a m", p=P)).then_inc(w_o, 16)

            def load_ffn(layer):
                sp.dma_start(W1[:, :, :], l_w1[layer].rearrange("(k p) n -> p k n", p=P)).then_inc(w_1, 16)
                w2 = l_w2[layer]
                sp.dma_start(W2[:, 0:MT - 1, :], w2[0:(MT - 1) * P, :].rearrange("(m p) n -> p m n", p=P)).then_inc(w_2, 16)
                sp.dma_start(W2[0:MLAST, MT - 1, :], w2[(MT - 1) * P:HID, :]).then_inc(w_2, 16)

            def load_qkv(layer):
                for half in range(2):
                    for kind in range(3):
                        last = max(c for c, (k_, _, h_) in enumerate(CHUNKS) if (k_, h_) == (kind, half))
                        sp.wait_ge(pe_q, least(NCH * (SEQS * (layer + 1) - 1) + last + 1))
                        at = kind * INNER + half * HALF
                        for k in range(KD):
                            sp.dma_start(Wqkv[:, k, kind, half * HALF:(half + 1) * HALF],
                                         l_wqkv[layer, k * P:(k + 1) * P, at:at + HALF]).then_inc(w_q[3 * half + kind], 16)

            for half in range(2):
                for kind, src in enumerate((wq, wk, wv)):
                    for k in range(KD):
                        sp.dma_start(Wqkv[:, k, kind, half * HALF:(half + 1) * HALF].rearrange("p (h d) -> p h d", d=DH),
                                     src[half * 8:half * 8 + 8, k * P:(k + 1) * P, :].rearrange("h p d -> p h d")
                                     ).then_inc(w_q[3 * half + kind], 16)
            load_wo(wo)
            sp.wait_ge(v_em, SEQS)
            load_ffn(0)
            load_qkv(0)
            sp.wait_ge(pe_wo, SEQS)
            load_wo(l_wo[0])
            with sp.Fori(1, DEPTH) as layer:
                load_qkv(layer)
                sp.wait_ge(pe_wo, SEQS * (layer + 1))
                load_wo(l_wo[layer])
                sp.wait_ge(pe_w2, SEQS * layer)
                load_ffn(layer)
            def store(s):
                sp.wait_ge(a_y, s + 1)
                sp.dma_start(out[s].rearrange("(t p) c -> p t c", p=P), yo[:, :, :]).then_inc(s_out, 16)
            sequences(sp, store)
            sp.wait_ge(s_out, 16 * SEQS)

        N_CONST = 16 * 9

        @block.tensor
        def _(pe):
            mm = nc.tensor.matmul
            held = {}

            def take(bank, *read):
                for s, value in held[bank.name]:
                    pe.wait_ge(s, value)
                held[bank.name] = [read]
                return bank

            def project(b, c):
                kind, t, half = CHUNKS[c]
                ps = take(A[c % 2], a_q, NCH * b.n_q + c + 1)
                if c == 0:
                    pe.wait_ge(v_xs, b.n_q + 1)
                layer = 0 if b.q.kind == "G" else b.q.layer + 1
                if t == 0:
                    pe.wait_ge(w_q[3 * half + kind], 32 * (layer + 1))
                cols = slice(half * HALF, (half + 1) * HALF)
                if b.q.kind == "G":
                    mm(ps[:, :], ones1[:, :], bQKV[:, kind, cols], start=True, stop=False)
                for k in range(KD):
                    last = mm(ps[:, :], xs[:, k, t * P:(t + 1) * P], Wqkv[:, k, kind, cols],
                              start=(k == 0 and b.q.kind == "L"), stop=(k == KD - 1))
                last.then_inc(pe_q, 1)

            def turn_qk(b, u):
                half = u // 2
                n_before = b.n_a + 1
                n = UNITS * b.n_a + u + 1
                if u % 2 == 0 and b.a.kind == "G":
                    pe.wait_ge(g_add, least(8 * n_before - (4 if half == 0 else 0)))
                elif u % 2 == 0:
                    pe.wait_ge(g_rot, least(8 * (n_before - SEQS) - (4 if half == 0 else 0)))
                for kind, done, read in ((0, pe_tq, a_qT), (1, pe_tk, v_kT)):
                    ps = take(T[kind], read, n)
                    for a in range(2):
                        pair = 2 * u + a
                        for t in range(TT):
                            last = nc.tensor.transpose(ps[:, a * SEQ + t * P:a * SEQ + (t + 1) * P],
                                                       qr[:, t, kind, pair * P:(pair + 1) * P], idf[:, :])
                    last.then_inc(done, 1)

            def scores(b, u):
                n = UNITS * b.n_a + u
                causal = b.a.kind == "G"
                m0 = 0 if causal else P + SEQ
                w1 = SEQ if causal else SEQ - WINDOW
                pe.wait_ge(a_qT, n + 1)
                pe.wait_ge(v_kT, n + 1)
                pe.wait_ge(a_x0, n)
                mm(S0[:, :], idb[:, :], mk[:, None, m0:m0 + P].to_broadcast((P, 4, P)), start=True, stop=False)
                for a in range(2):
                    last = mm(S0[:, a * SEQ:(a + 1) * SEQ], qT[:, u % 2, a, 0:P], kT[:, u % 2, a, :, 0:P],
                              start=False, stop=(a == 1))
                last.then_inc(pe_s0, 1)
                pe.wait_ge(a_x1, n)
                for a in range(2):
                    mm(S1[:, a, 0:2 * w1], idb[:, :], mk[:, None, m0 + P:m0 + P + w1].to_broadcast((P, 2, w1)),
                       start=True, stop=False)
                    last = mm(S1[:, a, 0:2 * w1], qT[:, u % 2, a, P:SEQ], kT[:, u % 2, a, :, SEQ - w1:SEQ],
                              start=False, stop=True)
                last.then_inc(pe_s1, 1)

            def turn_p(b, u, pair):
                rows = P if b.a.kind == "G" else WINDOW
                for h in (2 * pair, 2 * pair + 1):
                    pe.wait_ge(g_p, 16 * b.n_a + 4 * u + h + 1)
                    ps = take(T[h % 2], a_pt, 16 * b.n_a + 4 * u + h + 1)
                    nc.tensor.transpose(ps[:, 0:P], Pr[:, 1, h, P:SEQ], idf[:, :])
                    nc.tensor.transpose(ps[:, P:2 * P], Pr[:, 0, h, 0:P], idf[:, :])
                    nc.tensor.transpose(ps[:, 2 * P:2 * P + rows], Pr[0:rows, 1, h, 0:P], idf[0:rows, 0:rows]
                                        ).then_inc(pe_pt, 1)

            def values(b, u):
                pe.wait_ge(v_ot, UNITS * b.n_a + u)
                for h in range(4):
                    a, e = h // 2, h % 2
                    cols = slice((4 * u + h) * DH, (4 * u + h + 1) * DH)
                    pe.wait_ge(a_pt, 16 * b.n_a + 4 * u + h + 1)
                    mm(O[e * DH:(e + 1) * DH, a * SEQ:(a + 1) * SEQ], V[:, 0, cols], PT[:, h, P:P + SEQ],
                       start=True, stop=False)
                    last = mm(O[e * DH:(e + 1) * DH, a * SEQ + P:(a + 1) * SEQ], V[:, 1, cols], PT[:, h, 0:P],
                              start=False, stop=True)
                last.then_inc(pe_o, 1)

            def out_project(b):
                layer = 0 if b.a.kind == "G" else b.a.layer + 1
                ps = take(A[0], v_res, b.n_a + 1)
                pe.wait_ge(w_o, 16 * (layer + 1))
                pe.wait_ge(v_ot, UNITS * (b.n_a + 1))
                for m in range(KD):
                    for a in range(PAIRS):
                        last = mm(ps[:, m * SEQ:(m + 1) * SEQ], Wo[:, a, m * P:(m + 1) * P], OT[:, a, :],
                                  start=(a == 0), stop=(a == PAIRS - 1))
                last.then_inc(pe_wo, 1)

            def ln_mean(b, ready):
                ps = take(A[0], v_ln, N_LN * b.n_ln + 1)
                pe.wait_ge(*ready)
                for k in range(KD):
                    last = mm(ps[:, 0:SEQ], onesN[:, :], xf[:, k, :], start=(k == 0), stop=(k == KD - 1))
                last.then_inc(pe_ln, 1)

            def ln_var(b):
                ps = take(A[1], v_ln, N_LN * b.n_ln + 2)
                pe.wait_ge(a_sq, b.n_ln + 1)
                for k in range(KD):
                    last = mm(ps[:, 0:SEQ], onesN[:, :], sqF[:, k, :], start=(k == 0), stop=(k == KD - 1))
                last.then_inc(pe_ln, 1)

            def up(b, slot):
                ps = take(A[UP_BANK[slot]], *((a_gelu, 3 * b.n_f + slot + 1) if slot < 3 else (v_hid, 3 * b.n_f + slot - 2)))
                if slot == 0:
                    pe.wait_ge(w_1, 16 * (b.f.layer + 1))
                    pe.wait_ge(v_xn, b.n_ln + 1)
                base = HID if slot < 3 else 0
                for m in (2 * (slot % 3), 2 * (slot % 3) + 1):
                    n = P if m < MT - 1 else MLAST
                    for k in range(KD):
                        last = mm(ps[0:n, (m % 2) * SEQ:(m % 2 + 1) * SEQ], W1[:, k, base + m * P:base + m * P + n],
                                  xn[:, k, :], start=(k == 0), stop=(k == KD - 1))
                last.then_inc(pe_w1, 1)

            def down(b):
                ps = take(A[1], v_out, b.n_f + 1)
                pe.wait_ge(w_2, 32 * (b.f.layer + 1))
                pe.wait_ge(v_hid, 3 * (b.n_f + 1))
                for o in range(KD):
                    for m in range(MT):
                        n = P if m < MT - 1 else MLAST
                        last = mm(ps[:, o * SEQ:(o + 1) * SEQ], W2[0:n, m, o * P:(o + 1) * P], G[0:n, m, :],
                                  start=(m == 0), stop=(m == MT - 1))
                last.then_inc(pe_w2, 1)

            def body(b):
                held["A0"] = held["A1"] = [(a_q, NCH * b.n_q), (v_out, b.n_f), (v_res, b.n_a),
                                           (v_ln, N_LN * b.n_ln - (N_LN - 2))]
                held["T0"] = held["T1"] = [(a_pt, 16 * b.n_a)]
                ffn = b.f is not None and b.f.kind == "L"
                if b.a:
                    if b.a.kind == "L" and isinstance(b.n_a, int) and b.n_a == SEQS:
                        pe.wait_ge(pad_ready, 2)
                    turn_qk(b, 0)
                    turn_qk(b, 1)
                if b.f:
                    ln_mean(b, (v_xf, b.n_ln - SEQS + 1))
                if b.a:
                    scores(b, 0)
                if b.f:
                    ln_var(b)
                if b.q:
                    for c in (0, 1, 2):
                        project(b, c)
                if b.a:
                    turn_p(b, 0, 0)
                if b.q:
                    project(b, 3)
                if b.a:
                    turn_p(b, 0, 1)
                    scores(b, 1)
                    values(b, 0)
                if ffn:
                    for slot in (0, 1, 2):
                        up(b, slot)
                if b.a:
                    turn_qk(b, 2)
                    turn_p(b, 1, 0)
                if ffn:
                    up(b, 3)
                if b.a:
                    turn_p(b, 1, 1)
                    scores(b, 2)
                    values(b, 1)
                if b.q:
                    project(b, 4)
                    project(b, 5)
                if b.a:
                    turn_qk(b, 3)
                if b.q:
                    project(b, 6)
                if ffn:
                    up(b, 4)
                if b.a:
                    turn_p(b, 2, 0)
                if ffn:
                    up(b, 5)
                if b.a:
                    turn_p(b, 2, 1)
                    scores(b, 3)
                    values(b, 2)
                if b.q:
                    project(b, 7)
                    project(b, 8)
                if b.a:
                    turn_p(b, 3, 0)
                if b.q:
                    project(b, 9)
                if b.a:
                    turn_p(b, 3, 1)
                    values(b, 3)
                if b.q:
                    project(b, 10)
                if ffn:
                    down(b)
                if b.a:
                    out_project(b)
                if b.q:
                    project(b, 11)

            pe.wait_ge(s_const, N_CONST)
            pe.wait_ge(zeroed, 6)
            def embed(s):
                pe.wait_ge(v_em, s + 1)
                pe.wait_ge(a_e, s)
                for k in range(KD):
                    for t in range(TT):
                        last = nc.tensor.transpose(T[0][:, k * SEQ + t * P:k * SEQ + (t + 1) * P],
                                                   em[:, t, k * P:(k + 1) * P], idf[:, :])
                last.then_inc(pe_e, 1)
                held["A0"] = held["A1"] = [(v_ln, N_LN * s)]
                b = Body(None, None, None, 0, 0, 0, s)
                ln_mean(b, (a_e, s + 1))
                ln_var(b)
            sequences(pe, embed)
            pe.wait_ge(v_ln, N_LN * SEQS)
            bodies(pe, body)
            def restore(s):
                pe.wait_ge(v_y, s + 1)
                pe.wait_ge(a_y, s)
                for t in range(TT):
                    for k in range(KD):
                        last = nc.tensor.transpose(T[0][:, t * DIM + k * P:t * DIM + (k + 1) * P],
                                                   yb[:, k, t * P:(t + 1) * P], idf[:, :])
                last.then_inc(pe_y, 1)
            sequences(pe, restore)

        @block.scalar
        def _(act):
            f = nc.scalar.activation

            def evac_chunk(b, c):
                kind, t, half = CHUNKS[c]
                ps = A[c % 2]
                act.wait_ge(pe_q, NCH * b.n_q + c + 1)
                if kind == 2:
                    act.wait_ge(pe_o, UNITS * b.n_a + (2 * (half + 1) if b.a else 0))
                    f(V[:, t, half * HALF:(half + 1) * HALF], ps[:, :], ACT.Copy).then_inc(a_q, 1)
                    return
                slot = QK_SLOT.index(c)
                act.wait_ge(v_rot, least(8 * b.n_q + slot - 1))
                if b.q.kind == "L":
                    f(sq[:, slot % 2, :], ps[:, :], ACT.Square)
                f(raw[:, slot % 2, :], ps[:, :], ACT.Copy).then_inc(a_q, 1)

            def evac_q(b, u):
                n = UNITS * b.n_a + u
                act.wait_ge(pe_tq, n + 1)
                act.wait_ge(pe_s1, least(n - 1))
                f(qT[:, u % 2, :, :], T[0][:, :].rearrange("p (a q) -> p a q", a=2), ACT.Copy).then_inc(a_qT, 1)

            def exps(b, u):
                n = UNITS * b.n_a + u
                w1 = SEQ if b.a.kind == "G" else SEQ - WINDOW
                act.wait_ge(pe_pt, 4 * n)
                act.wait_ge(v_max, 2 * n + 1)
                for h in range(4):
                    last = f(Pr[:, 0, h, 0:P], S0[:, h * P:(h + 1) * P], ACT.Exp, bias=nm[:, u % 2, h:h + 1],
                             accum_out=rs[:, u % 2, h:h + 1])
                last.then_inc(a_x0, 1)
                act.wait_ge(v_max, 2 * n + 2)
                for h in range(4):
                    last = f(Pr[:, 1, h, SEQ - w1:SEQ], S1[:, h // 2, (h % 2) * w1:(h % 2 + 1) * w1], ACT.Exp,
                             bias=nm[:, u % 2, 4 + h:5 + h], accum_out=rs[:, u % 2, 4 + h:5 + h])
                last.then_inc(a_x1, 1)

            def evac_p(b, u, pair):
                width = P + SEQ if b.a.kind == "G" else 2 * P + WINDOW
                for h in (2 * pair, 2 * pair + 1):
                    act.wait_ge(pe_pt, 16 * b.n_a + 4 * u + h + 1)
                    act.wait_ge(pe_o, UNITS * b.n_a + u)
                    f(PT[:, h, 0:width], T[h % 2][:, 0:width], ACT.Copy).then_inc(a_pt, 1)

            def squares(b):
                act.wait_ge(v_ln, N_LN * b.n_ln + 1)
                act.wait_ge(pe_ln, 2 * b.n_ln)
                f(sqF[:, :, :], xc[:, :, :], ACT.Square).then_inc(a_sq, 1)

            def gelus(b):
                for slot in range(3):
                    act.wait_ge(pe_w1, 6 * b.n_f + slot + 1)
                    act.wait_ge(pe_w2, b.n_f)
                    act.wait_ge(v_bG, b.n_f + 1)
                    for m in (2 * slot, 2 * slot + 1):
                        n = P if m < MT - 1 else MLAST
                        last = f(G[0:n, m, :], A[UP_BANK[slot]][0:n, (m % 2) * SEQ:(m % 2 + 1) * SEQ], ACT.Gelu,
                                 bias=bG[0:n, m:m + 1])
                    last.then_inc(a_gelu, 1)

            def body(b):
                if b.a:
                    evac_q(b, 0)
                    evac_q(b, 1)
                if b.f:
                    squares(b)
                if b.a:
                    exps(b, 0)
                if b.q:
                    for c in (0, 1, 2):
                        evac_chunk(b, c)
                if b.a:
                    evac_p(b, 0, 0)
                if b.q:
                    evac_chunk(b, 3)
                if b.a:
                    evac_p(b, 0, 1)
                    exps(b, 1)
                if b.f and b.f.kind == "L":
                    gelus(b)
                if b.a:
                    evac_q(b, 2)
                    evac_p(b, 1, 0)
                    evac_p(b, 1, 1)
                    exps(b, 2)
                if b.q:
                    evac_chunk(b, 4)
                    evac_chunk(b, 5)
                if b.a:
                    evac_q(b, 3)
                if b.q:
                    evac_chunk(b, 6)
                if b.a:
                    evac_p(b, 2, 0)
                    evac_p(b, 2, 1)
                    exps(b, 3)
                if b.q:
                    evac_chunk(b, 7)
                    evac_chunk(b, 8)
                if b.a:
                    evac_p(b, 3, 0)
                if b.q:
                    evac_chunk(b, 9)
                if b.a:
                    evac_p(b, 3, 1)
                if b.q:
                    evac_chunk(b, 10)
                    evac_chunk(b, 11)

            act.wait_ge(s_const, N_CONST)
            def embed(s):
                act.wait_ge(pe_e, s + 1)
                ps = T[0][:, :].rearrange("p (k q) -> p k q", k=KD)
                act.wait_ge(pe_ln, 2 * s)
                act.wait_ge(v_ln, N_LN * s)
                f(xf[:, :, :], ps, ACT.Copy)
                f(hT[:, :, ds(s, 1), :], ps[:, :, None, :], ACT.Copy).then_inc(a_e, 1)
                squares(Body(None, None, None, 0, 0, 0, s))
            sequences(act, embed)
            bodies(act, body)
            def restore(s):
                act.wait_ge(pe_y, s + 1)
                act.wait_ge(s_out, 16 * s)
                f(yo[:, :, :], T[0][:, :].rearrange("p (t c) -> p t c", t=TT), ACT.Copy).then_inc(a_y, 1)
            sequences(act, restore)

        @block.vector
        def _(dve):
            v = nc.vector
            MAGIC = float(0x5F3759DF)

            def chain(s, base):
                n = [0]

                def link(ins):
                    n[0] += 1
                    ins.then_inc(s, 1)
                    dve.wait_ge(s, base + n[0])
                return link

            def newton(x, y, t, link):
                link(v.tensor_scalar(t.bitcast(i32), x.bitcast(i32), 1, None, ALU.logical_shift_right))
                link(v.tensor_scalar(y.bitcast(i32), t.bitcast(i32), -1.0, MAGIC, ALU.mult, ALU.add))
                for i in range(3):
                    link(v.scalar_tensor_tensor(t, y, -0.5, y, ALU.mult, ALU.mult))
                    link(v.tensor_tensor(t, t, x, ALU.mult))
                    last = v.scalar_tensor_tensor(y, t, 1.5, y, ALU.add, ALU.mult)
                    if i < 2:
                        link(last)
                return last

            def copy(to, of):
                return v.tensor_scalar(to, of, 1.0, None, ALU.mult)

            def take_input(b):
                s = b.q.seq
                dve.wait_ge(pe_q, NCH * b.n_q)
                if b.q.kind == "G":
                    copy(xs[:, :, None, :], xT[:, :, ds(s, 1), 1:SEQ + 1]).then_inc(v_xs, 1)
                    return
                if isinstance(b.q.layer, int):
                    dve.wait_ge(v_xn, SEQS + s + 1)
                else:
                    dve.wait_ge(v_out, least(b.n_q - 2 * SEQS + 1))
                copy(xs[:, 0, None, :], xT[:, 0, ds(s, 1), 1:SEQ + 1])
                copy(xs[:, 1, None, :], xT[:, 1, ds(s, 1), 0:SEQ]).then_inc(v_xs, 1)

            def layer_tables(b):
                L = ds(b.q.layer, 1)
                n = 0
                for kind in range(2):
                    c, sn = 2 * kind, 2 * kind + 1
                    w = qks[:, L, kind, :].to_broadcast((P, TT, DH))
                    v.tensor_tensor(tabL[:, :, c, :], tabB[:, :, c, :], w, ALU.mult)
                    for x in range(2):
                        to, of = slice(32 * x, 32 * x + 32), slice(32 - 32 * x, 64 - 32 * x)
                        w = qks[:, L, kind, of].to_broadcast((P, TT, 32))
                        last = v.tensor_tensor(tabL[:, :, sn, to], tabB[:, :, sn, to], w, ALU.mult)
                last.then_inc(v_tab, 1)
                dve.wait_ge(v_tab, b.q.layer + 1)

            def gate_biases(b):
                dve.wait_ge(a_gelu, 3 * b.n_f)
                copy(bG[:, None, :], par[:, ds(b.f.layer, 1), 10:10 + MT]).then_inc(v_bG, 1)

            def copy_f(b):
                s = b.f.seq
                dve.wait_ge(pe_ln, 2 * b.n_ln)
                dve.wait_ge(v_res, least(b.n_ln - SEQS + 1))
                if b.f.kind == "G":
                    copy(xf[:, :, None, :], hT[:, :, ds(s, 1), :]).then_inc(v_xf, 1)
                else:
                    copy(xf[:, 0, None, :], xT[:, 0, ds(s, 1), 1:SEQ + 1])
                    copy(xf[:, 1, None, :], xT[:, 1, ds(s, 1), 0:SEQ]).then_inc(v_xf, 1)

            def evac_k(b, u):
                n = UNITS * b.n_a + u
                dve.wait_ge(pe_tk, n + 1)
                dve.wait_ge(pe_s1, least(n - 1))
                for e in range(2):
                    rows = slice(e * DH, (e + 1) * DH)
                    last = v.tensor_copy(kT[rows, u % 2, :, e, :], T[1][rows, :].rearrange("p (a q) -> p a q", a=2))
                last.then_inc(v_kT, 1)

            def maxima(b, u):
                n = UNITS * b.n_a + u
                w1 = SEQ if b.a.kind == "G" else SEQ - WINDOW
                dve.wait_ge(pe_s0, n + 1)
                v.tensor_reduce(nm[:, u % 2, 0:4], S0[:, :].rearrange("p (h k) -> p h k", h=4), axis=AX.X,
                                op=ALU.max, negate=True).then_inc(v_max, 1)
                dve.wait_ge(pe_s1, n + 1)
                v.tensor_reduce(nm[:, u % 2, 4:8], S1[:, :, 0:2 * w1].rearrange("p a (h k) -> p a h k", h=2),
                                axis=AX.X, op=ALU.max, negate=True).then_inc(v_max, 1)

            def reciprocals(b, u):
                n = UNITS * b.n_a + u
                dve.wait_ge(a_x1, n + 1)
                v.reciprocal(rr[:, u % 2, :], rs[:, u % 2, :]).then_inc(v_rec, 1)

            def rotate(b, slot):
                c = QK_SLOT[slot]
                kind, t, half = CHUNKS[c]
                tab = tabG if b.q.kind == "G" else tabL
                dve.wait_ge(a_q, NCH * b.n_q + c + 1)
                if b.q.kind == "L":
                    i = slot % 4
                    v.tensor_reduce(ssq[:, i * 8:(i + 1) * 8], sq[:, slot % 2, :].rearrange("p (h d) -> p h d", d=DH),
                                    axis=AX.X, op=ALU.add)
                dve.wait_ge(pe_tk, UNITS * b.n_a + (2 * (half + 1) if b.a else 0))
                r = raw[:, slot % 2, :]
                v.tensor_tensor(qr[:, t, kind, half * HALF:(half + 1) * HALF].rearrange("p (h d) -> p h d", d=DH),
                                r.rearrange("p (h d) -> p h d", d=DH),
                                tab[:, t, 2 * kind, :][:, None, :].to_broadcast((P, 8, DH)), ALU.mult)
                dve.wait_ge(g_add, least(8 * b.n_q + slot - 1))
                v.tensor_tensor(t2[:, slot % 2, :].rearrange("p (h x d) -> p h x d", x=2, d=32),
                                r.rearrange("p (h x d) -> p h x d", x=2, d=32)[:, :, ::-1, :],
                                tab[:, t, 2 * kind + 1, :].rearrange("p (x d) -> p x d", x=2)[:, None, :, :]
                                .to_broadcast((P, 8, 2, 32)), ALU.mult).then_inc(v_rot, 1)

            def norms(b, half):
                if b.q.kind == "G":
                    return
                n = 2 * (b.n_q - SEQS) + half
                link = chain(v_nrm, N_NEWTON * n)
                dve.wait_ge(v_rot, 8 * b.n_q + 4 * half + 4)
                dve.wait_ge(g_rot, 4 * n)
                link(v.tensor_scalar(ssq[:, :], ssq[:, :], 1e-24, None, ALU.max))
                newton(ssq[:, :], rn[:, :], nt[:, :], link).then_inc(v_rn, 1)

            def centre(b):
                n = b.n_ln
                dve.wait_ge(pe_ln, 2 * n + 1)
                dve.wait_ge(a_sq, n)
                v.tensor_tensor(xc[:, :, :], xf[:, :, :], A[0][:, None, 0:SEQ].to_broadcast((P, KD, SEQ)),
                                ALU.subtract).then_inc(v_ln, 1)

            def normalise(b):
                n = b.n_ln
                link = chain(v_ln, N_LN * n + 1)
                dve.wait_ge(pe_ln, 2 * n + 2)
                link(v.tensor_scalar(vr[:, :], A[1][:, 0:SEQ], 1e-5, None, ALU.add))
                link(newton(vr[:, :], ry[:, :], rt[:, :], link))
                dve.wait_ge(pe_w1, 6 * b.n_f)
                link(v.tensor_tensor(xn[:, :, :], xc[:, :, :], ry[:, None, :].to_broadcast((P, KD, SEQ)), ALU.mult))
                if b.f.kind == "G":
                    copy(xT[:, :, ds(b.f.seq, 1), 1:SEQ + 1], xn[:, :, None, :]).then_inc(v_xn, 1)
                    return
                for k in range(KD):
                    last = v.tensor_scalar(xn[:, k, :], xn[:, k, :], par[:, ds(b.f.layer, 1), k],
                                           par[:, ds(b.f.layer, 1), 2 + k], ALU.mult, ALU.add)
                last.then_inc(v_xn, 1)

            def evac_o(b, u):
                n = UNITS * b.n_a + u
                dve.wait_ge(pe_o, n + 1)
                dve.wait_ge(pe_wo, b.n_a)
                v.tensor_copy(OT[:, 2 * u:2 * u + 2, :], O[:, :].rearrange("p (a q) -> p a q", a=2)).then_inc(v_ot, 1)

            def hidden(b, slot):
                dve.wait_ge(pe_w1, 6 * b.n_f + slot + 1)
                dve.wait_ge(a_gelu, 3 * b.n_f + slot - 2)
                for m in (2 * (slot - 3), 2 * (slot - 3) + 1):
                    n = P if m < MT - 1 else MLAST
                    last = v.scalar_tensor_tensor(
                        G[0:n, m, :], A[UP_BANK[slot]][0:n, (m % 2) * SEQ:(m % 2 + 1) * SEQ],
                        par[0:n, ds(b.f.layer, 1), 4 + m], G[0:n, m, :], ALU.add, ALU.mult)
                last.then_inc(v_hid, 1)

            def add_attention(b):
                dve.wait_ge(pe_wo, b.n_a + 1)
                s = b.a.seq
                if b.a.kind == "G":
                    for k in range(KD):
                        h = hT[:, k, ds(s, 1), :]
                        last = v.scalar_tensor_tensor(h, A[0][:, None, k * SEQ:(k + 1) * SEQ], bO[:, k:k + 1], h,
                                                      ALU.add, ALU.add)
                else:
                    x = xT[:, :, ds(s, 1), 1:SEQ + 1]
                    last = v.tensor_tensor(x, x, A[0][:, :].rearrange("p (k o q) -> p k o q", k=KD, o=1), ALU.add)
                last.then_inc(v_res, 1)

            def add_ffn(b):
                dve.wait_ge(pe_w2, b.n_f + 1)
                for k in range(KD):
                    x = xT[:, k, ds(b.f.seq, 1), 1:SEQ + 1]
                    last = v.scalar_tensor_tensor(x, A[1][:, None, k * SEQ:(k + 1) * SEQ],
                                                  par[:, ds(b.f.layer, 1), 16 + k], x, ALU.add, ALU.add)
                last.then_inc(v_out, 1)

            def body(b):
                ffn = b.f is not None and b.f.kind == "L"
                if b.q and b.q.kind == "L" and isinstance(b.q.seq, int) and b.q.seq == 0:
                    layer_tables(b)
                if b.q:
                    take_input(b)
                if b.f:
                    copy_f(b)
                if ffn:
                    gate_biases(b)
                if b.a:
                    evac_k(b, 0)
                    evac_k(b, 1)
                if b.f:
                    centre(b)
                if b.a:
                    maxima(b, 0)
                if b.f:
                    normalise(b)
                if b.a:
                    reciprocals(b, 0)
                if b.q:
                    rotate(b, 0)
                    rotate(b, 1)
                if b.a:
                    maxima(b, 1)
                    evac_o(b, 0)
                if b.q:
                    rotate(b, 2)
                if b.a:
                    reciprocals(b, 1)
                if b.q:
                    rotate(b, 3)
                    norms(b, 0)
                if b.a:
                    evac_k(b, 2)
                    maxima(b, 2)
                    evac_o(b, 1)
                if ffn:
                    hidden(b, 3)
                if b.a:
                    evac_k(b, 3)
                    reciprocals(b, 2)
                if b.q:
                    rotate(b, 4)
                if ffn:
                    hidden(b, 4)
                    hidden(b, 5)
                if b.a:
                    maxima(b, 3)
                    evac_o(b, 2)
                if b.q:
                    rotate(b, 5)
                if b.a:
                    reciprocals(b, 3)
                if b.q:
                    rotate(b, 6)
                    rotate(b, 7)
                if b.a:
                    evac_o(b, 3)
                if b.q:
                    norms(b, 1)
                if ffn:
                    add_ffn(b)
                if b.a:
                    add_attention(b)

            v.memset(onesN[:, :], 1.0 / DIM).then_inc(zeroed, 1)
            v.memset(ones1[:, :], 1.0).then_inc(zeroed, 1)
            v.memset(xT[:, :, :, 0:1], 0.0).then_inc(zeroed, 1)
            dve.wait_ge(s_const, N_CONST)
            dve.wait_ge(zeroed, 6)
            dve.wait_ge(s_gat, 16 * 2 * SEQS * TT)
            def embed(s):
                u = gu[:, ds(s * TT, TT), :]
                v.tensor_scalar(u, u, KEEP, float(np.float32(1) / np.float32(KEEP)), ALU.is_lt, ALU.mult).then_inc(v_emb, 1)
                dve.wait_ge(v_emb, s + 1)
                dve.wait_ge(pe_e, s)
                v.tensor_tensor(em[:, :, :], gw[:, ds(s * TT, TT), :], u, ALU.mult).then_inc(v_em, 1)
                b = Body(None, None, Stage("G", s, 0), 0, 0, 0, s)
                dve.wait_ge(a_e, s + 1)
                centre(b)
                normalise(b)
            sequences(dve, embed)
            dve.wait_ge(v_xn, SEQS)
            bodies(dve, body)
            dve.wait_ge(v_out, SEQS * DEPTH)
            def restore(s):
                dve.wait_ge(pe_y, s)
                v.tensor_tensor(yb[:, :, None, :], hT[:, :, ds(s, 1), :], xT[:, :, ds(s, 1), 1:SEQ + 1],
                                ALU.add).then_inc(v_y, 1)
            sequences(dve, restore)

        @block.gpsimd
        def _(pool):
            p = nc.gpsimd

            def scale_p(b, u):
                w1 = SEQ if b.a.kind == "G" else SEQ - WINDOW
                pool.wait_ge(v_rec, UNITS * b.n_a + u + 1)
                for h in range(4):
                    x, y = Pr[:, 0, h, 0:P], Pr[:, 1, h, SEQ - w1:SEQ]
                    if h == 0:
                        p.tensor_tensor(x, x, rr[:, u % 2, h:h + 1].to_broadcast((P, P)), ALU.mult)
                    else:
                        p.tensor_scalar(x, x, rr[:, u % 2, h:h + 1], 1.0, ALU.mult, ALU.mult)
                    p.tensor_scalar(y, y, rr[:, u % 2, 4 + h:5 + h], 1.0, ALU.mult, ALU.mult).then_inc(g_p, 1)

            def chunk(slot):
                kind, t, half = CHUNKS[QK_SLOT[slot]]
                return qr[:, t, kind, half * HALF:(half + 1) * HALF]

            def add_turned(b, slot):
                pool.wait_ge(v_rot, 8 * b.n_q + slot + 1)
                p.tensor_tensor(chunk(slot), chunk(slot), t2[:, slot % 2, :], ALU.add).then_inc(g_add, 1)

            def scale_qk(b, slots):
                if b.q.kind == "G":
                    return
                for slot in slots:
                    pool.wait_ge(v_rn, 2 * (b.n_q - SEQS) + slot // 4 + 1)
                    i = slot % 4
                    x = chunk(slot).rearrange("p (h d) -> p h d", d=DH)
                    pool.wait_ge(g_add, 8 * b.n_q + slot + 1)
                    p.tensor_tensor(x, x, rn[:, i * 8:(i + 1) * 8, None].to_broadcast((P, 8, DH)),
                                    ALU.mult).then_inc(g_rot, 1)

            def clear_padding(kind):
                if kind == "L":
                    pool.wait_ge(pe_pt, 16 * SEQS)
                    pool.wait_ge(pe_o, UNITS * SEQS)
                done = zeroed if kind == "G" else pad_ready
                p.memset(Pr[:, 1, :, 0:WINDOW], 0.0).then_inc(done, 1)
                p.memset(PT[:, :, 2 * P + WINDOW:P + SEQ], 0.0).then_inc(done, 1)

            def body(b):
                if b.a:
                    if b.a.kind == "L" and isinstance(b.n_a, int) and b.n_a == SEQS:
                        clear_padding("L")
                    scale_p(b, 0)
                if b.q:
                    add_turned(b, 0)
                    add_turned(b, 1)
                if b.a:
                    scale_p(b, 1)
                if b.q:
                    add_turned(b, 2)
                    add_turned(b, 3)
                    scale_qk(b, (0, 1))
                if b.a:
                    scale_p(b, 2)
                if b.q:
                    scale_qk(b, (2, 3))
                    add_turned(b, 4)
                if b.a:
                    scale_p(b, 3)
                if b.q:
                    add_turned(b, 5)
                    add_turned(b, 6)
                    add_turned(b, 7)
                    scale_qk(b, (4, 5, 6, 7))

            p.memset(kT[:, :, :, :, :], 0.0).then_inc(zeroed, 1)
            clear_padding("G")
            pool.wait_ge(s_ids, 16)
            for t in range(SEQS * TT):
                for table, to in ((emb_w, gw), (emb_u, gu)):
                    p.indirect_dma_start(out=to[:, t, :], out_offset=None, in_=table[:, :],
                                         in_offset=bass.IndirectOffsetOnAxis(ap=idx[:, t:t + 1], axis=0)
                                         ).then_inc(s_gat, 16)
            bodies(pool, body)


def kernel(**inputs):
    import concourse.bacc as bacc
    from concourse.bass_utils import run_bass_kernel_spmd

    x = {k: np.ascontiguousarray(a) for k, a in inputs.items()}

    def halves(a, width):
        return a.reshape(DEPTH, -1, width).transpose(2, 0, 1)

    def tiles(a):
        padded = np.zeros((DEPTH, MT * P), a.dtype)
        padded[:, :HID] = a
        return halves(padded, P)

    b1 = x["L0_ffn_b1"]
    params = np.concatenate([halves(x["L0_ffn_ln_g"], P), halves(x["L0_ffn_ln_b"], P), tiles(b1[:, :HID]),
                             tiles(b1[:, HID:]), halves(x["L0_ffn_b2"], P)], 2)
    arrays = {
        "ids": x["x"].reshape(SEQS * TT, P).T,
        "emb_w": x["L0_tok_weight"], "emb_u": x["L0_tok_mask_u"],
        "wq": x["L0_attn_W_Q"], "wk": x["L0_attn_W_K"], "wv": x["L0_attn_W_V"],
        "bqkv": np.stack([x[f"L0_attn_b_{n}"].reshape(INNER) for n in "QKV"])[None],
        "wo": x["L0_attn_W_O"].reshape(INNER, DIM), "bo": x["L0_attn_b_O"].reshape(KD, P).T,
        "l_wqkv": x["L0_ffn_Wqkv"],
        "l_qk_scale": np.stack([x["L0_ffn_q_scale"], x["L0_ffn_k_scale"]], 1).reshape(1, -1),
        "l_wo": x["L0_ffn_Wo"], "l_par": params, "l_w1": x["L0_ffn_W1"], "l_w2": x["L0_ffn_W2"],
        **constants(),
    }
    nc = bacc.Bacc("TRN2", target_bir_lowering=False, num_devices=1)
    given, args = {}, {}
    for name, a in arrays.items():
        given[f"in_{name}"] = np.ascontiguousarray(a)
        args[name] = nc.dram_tensor(f"in_{name}", a.shape, mybir.dt.from_np(a.dtype), kind="ExternalInput").ap()
    out = nc.dram_tensor("out", (SEQS, SEQ, DIM), mybir.dt.float32, kind="ExternalOutput").ap()
    tower_kernel(nc, **args, out=out)
    result = run_bass_kernel_spmd(nc, [given], core_ids=[0])
    return result.results[0]["out"]
```

```python
from collections import namedtuple
from contextlib import ExitStack

import numpy as np
import concourse.bass as bass
from concourse import mybir
from concourse.alu_op_type import AluOpType as ALU

SEQS, SEQ, DIM = 8, 256, 256
HEADS, DH = 16, 64
DEPTH, WINDOW = 6, 64
INNER = HEADS * DH
HID = 682
P = 128
KD = DIM // P
TT = SEQ // P
HALF = INNER // 2
UNITS = 4
PAIRS = HEADS // 2
MT = -(-HID // P)
MLAST = HID - (MT - 1) * P
KEEP = 1.0 - 0.1

CHUNKS = [(kind, t, half) for half in range(2) for kind in range(3) for t in range(TT)]
NCH = len(CHUNKS)
QK_SLOT = [c for c, (kind, _, _) in enumerate(CHUNKS) if kind < 2]

UP_BANK = (0, 1, 0, 1, 1, 1)

N_NEWTON = 11
N_LN = 3 + N_NEWTON

Stage = namedtuple("Stage", "kind seq layer")
Body = namedtuple("Body", "q a f d n_q n_a n_f n_d n_ln")


def constants():
    f32 = np.float32
    half = np.arange(0, DH, 2, dtype=f32)
    pos = np.arange(SEQ, dtype=f32)

    def tables(angle, scale_q, scale_k, gain):
        cos, sin = np.cos(angle), np.sin(angle)
        sgn = np.where(np.arange(DH) < DH // 2, -1, 1).astype(f32)
        return np.stack([cos * scale_q * gain, sin * sgn * scale_q * gain,
                         cos * scale_k, sin * sgn * scale_k], 1).astype(f32)

    dim = np.arange(DH // 2, dtype=f32)
    freq = (f32(10000.0) ** (dim / f32(DH / 2))).astype(f32)
    freq = np.concatenate([freq, freq])
    tab_g = tables((pos[:, None] / freq[None]).astype(f32), 1, 1, 1 / 8)
    inv = (1.0 / f32(10000.0) ** (half / f32(DH))).astype(f32)
    ang = (pos[:, None] * inv[None]).astype(f32)
    ang = np.concatenate([ang, ang], -1)
    base = ((half + 0.4 * DH) / (1.4 * DH)).astype(f32)
    power = ((pos - SEQ // 2) / (WINDOW // 2)).astype(f32)
    scale = (base[None] ** power[:, None]).astype(f32)
    scale = np.concatenate([scale, scale], -1)
    tab_l = tables(ang, scale, (1 / scale).astype(f32), 8)

    def tiled(t):
        return np.ascontiguousarray(t.reshape(TT, P, 4, DH).transpose(1, 0, 2, 3))

    i, j = np.arange(SEQ)[:, None], np.arange(SEQ)[None]
    neg = f32(-1e30)
    causal = np.where(j <= i, f32(0), neg)
    local = np.where((j <= i) & (i <= j + WINDOW), f32(0), neg)
    bf16 = mybir.dt.np(mybir.dt.bfloat16)
    masks = np.concatenate([causal[:P, :P], causal[P:, :], local[:P, :P], local[P:, WINDOW:]], 1)
    return {"tab_g": tiled(tab_g), "tab_l": tiled(tab_l), "masks": masks.astype(bf16),
            "eye16": np.eye(P, dtype=f32).astype(bf16), "eye32": np.eye(P, dtype=f32)}


def tower_kernel(nc, ids, emb_w, emb_u, wq, wk, wv, bqkv, wo, bo, l_wqkv, l_qk_scale, l_wo, l_par,
                 l_w1, l_w2, tab_g, tab_l, masks, eye16, eye32, kept, out):
    f32, f32r, bf16, i32 = mybir.dt.float32, mybir.dt.float32r, mybir.dt.bfloat16, mybir.dt.int32
    ACT = mybir.ActivationFunctionType
    AX = mybir.AxisListType
    ds = bass.ds

    ctx = ExitStack()
    with ctx:
        def sb(name, shape, dt=f32):
            return ctx.enter_context(nc.sbuf_tensor(name, shape, dt))

        def pb(name):
            return ctx.enter_context(nc.psum_tensor(name, [P, 512], f32))

        def sem(name):
            return ctx.enter_context(nc.semaphore(name))

        xT = sb("xT", [P, KD, SEQS, SEQ + 1])
        Wh = sb("Wh", [P, KD, 3, INNER], f32r)
        with ExitStack() as raw_weights:
            Wraw = raw_weights.enter_context(nc.sbuf_tensor("Wraw", [P, KD, 3, INNER], f32))
        Wl = sb("Wl", [P, KD, 3, INNER], f32r)
        Wo = sb("Wo", [P, PAIRS, DIM])
        with ExitStack() as before_stack:
            gu = before_stack.enter_context(nc.sbuf_tensor("gu", [P, SEQS * TT, DIM], f32))
        W1h = sb("W1h", [P, KD, 2 * HID], f32r)
        W2 = sb("W2", [P, MT, DIM])
        with ExitStack() as before_stack:
            hT = before_stack.enter_context(nc.sbuf_tensor("hT", [P, KD, SEQS, SEQ], f32))
        with ExitStack() as raw_weights:
            W1raw = raw_weights.enter_context(nc.sbuf_tensor("W1raw", [P, KD, 2 * HID], f32))
        W1l = sb("W1l", [P, KD, 2 * HID], f32r)
        G = sb("G", [P, MT, SEQ])
        tabB = sb("tabB", [P, TT, 4, DH])
        tab = sb("tab", [P, TT, 4, DH])
        qks = sb("qks", [P, DEPTH, 2, DH])
        par = sb("par", [P, DEPTH, 18])
        bO = sb("bO", [P, KD])
        bQKV = sb("bQKV", [6, HALF])
        onesN = sb("onesN", [P, P])
        idb = sb("idb", [P, P], bf16)
        idf = sb("idf", [P, P])
        mk = sb("mk", [P, P + SEQ + P + SEQ - WINDOW], bf16)
        idx = sb("idx", [P, SEQS * TT], i32)
        xsh = sb("xsh", [P, KD, SEQ], f32r)
        xsl = sb("xsl", [P, KD, SEQ], f32r)
        raw = sb("raw", [P, 2, HALF])
        sq = sb("sq", [P, 2, HALF])
        t2 = sb("t2", [P, 2, HALF])
        qr = sb("qr", [P, TT, 2, INNER])
        ssq = sb("ssq", [P, 4 * 8])
        rn = sb("rn", [P, 4 * 8])
        nt = sb("nt", [P, 4 * 8])
        V = sb("V", [P, TT, INNER])
        qT = sb("qT", [P, 2, 2, SEQ])
        kT = sb("kT", [P, 2, 2, 2, SEQ])
        Pr = sb("Pr", [P, TT, 4, SEQ])
        nm = sb("nm", [P, 2, 8])
        rs = sb("rs", [P, 2, 8])
        rr = sb("rr", [P, 2, 8])
        PT = sb("PT", [P, 4, P + SEQ])
        OT = sb("OT", [P, PAIRS, SEQ])
        xf = sb("xf", [P, KD, SEQ])
        xc = sb("xc", [P, KD, SEQ])
        sqF = sb("sqF", [P, KD, SEQ])
        vr = sb("vr", [P, SEQ])
        ry = sb("ry", [P, TT])
        rt = sb("rt", [P, TT])
        bG = sb("bG", [P, MT])
        xnh = sb("xnh", [P, KD, SEQ], f32r)
        xnl = sb("xnl", [P, KD, SEQ], f32r)
        gw = qr[:, :, :, :].rearrange("p a b (c d) -> p (a b c) d", d=DIM)
        em = V[:, 0, 0:TT * DIM].rearrange("p (t c) -> p t c", c=DIM)
        hb = qr[:, :, :, :].rearrange("p a b (c d) -> p (a b c) d", d=SEQ).rearrange("p (k s) q -> p k s q", k=KD)
        yb, yo = xf, xc

        A = [pb("A0"), pb("A1")]
        T = [pb("T0"), pb("T1")]
        S0 = pb("S0")
        S1 = ctx.enter_context(nc.psum_tensor("S1", [P, 2, 512], f32))
        O = pb("O")

        s_keep, s_hb = sem("keep"), sem("hb")
        s_const, s_ids, s_gat, s_out = sem("const"), sem("ids"), sem("gather"), sem("out")
        w_q = [sem(f"w_q{j}") for j in range(6)]
        w_o, w_1, w_2 = sem("w_o"), sem("w_1"), sem("w_2")
        zeroed, pad_ready = sem("zeroed"), sem("pad_ready")
        pe_e, pe_y = sem("pe_e"), sem("pe_y")
        pe_q, pe_tq, pe_tk = sem("pe_q"), sem("pe_tq"), sem("pe_tk")
        pe_s0, pe_s1, pe_pt, pe_o, pe_wo = (sem(x) for x in ("pe_s0", "pe_s1", "pe_pt", "pe_o", "pe_wo"))
        pe_ln, pe_w1, pe_w2 = sem("pe_ln"), sem("pe_w1"), sem("pe_w2")
        a_e, a_y = sem("a_e"), sem("a_y")
        a_q, a_qT, a_x0, a_x1, a_pt, a_sq, a_gelu = (sem(x) for x in ("a_q", "a_qT", "a_x0", "a_x1", "a_pt", "a_sq", "a_gelu"))
        a_wh, a_w1h = sem("a_wh"), sem("a_w1h")
        v_em, v_y = sem("v_em"), sem("v_y")
        v_xs, v_kT, v_max, v_rec = sem("v_xs"), sem("v_kT"), sem("v_max"), sem("v_rec")
        v_rot, v_rn, v_ot, v_res = sem("v_rot"), sem("v_rn"), sem("v_ot"), sem("v_res")
        v_xf, v_ln, v_xn, v_hid, v_out = sem("v_xf"), sem("v_ln"), sem("v_xn"), sem("v_hid"), sem("v_out")
        v_nrm, v_tab, v_emb, v_bG = sem("v_nrm"), sem("v_tab"), sem("v_emb"), sem("v_bG")
        v_wl, v_w1l, v_aff = sem("v_wl"), sem("v_w1l"), sem("v_aff")
        g_add, g_rot, g_p = sem("g_add"), sem("g_rot"), sem("g_p")

        block = ctx.enter_context(nc.Block())

        def least(value):
            return max(value, 0) if isinstance(value, int) else value

        def bodies(eng, body):
            def g(q, a, f):
                body(Body(Stage("G", q, 0), None if a is None else Stage("G", a, 0),
                          None if f is None else Stage("G", f, 0), None,
                          q, 0 if a is None else a, 0, 0, SEQS + (0 if f is None else f)))

            def l(layer, s, before="L"):
                n = SEQS * layer + s
                prev = "L" if before == "L" else "G"
                if isinstance(s, int) and s == 0:
                    a, f = Stage(prev, SEQS - 1, layer - 1), Stage(prev, SEQS - 2, layer - 1)
                elif isinstance(s, int) and s == 1:
                    a, f = Stage("L", 0, layer), Stage(prev, SEQS - 1, layer - 1)
                else:
                    a, f = Stage("L", s - 1, layer), Stage("L", s - 2, layer)
                n_f = 0 if f.kind == "G" else n - 2
                if f.kind == "G" or (isinstance(n, int) and n == 2):
                    d, n_d = None, 0
                elif isinstance(s, int) and s < 3:
                    d, n_d = Stage("L", SEQS - 3 + s, layer - 1), n - 3
                else:
                    d, n_d = Stage("L", s - 3, layer), n - 3
                body(Body(Stage("L", s, layer), a, f, d, SEQS + n, SEQS + n - 1, n_f, n_d, 2 * SEQS + n - 2))

            g(0, None, None)
            g(1, 0, None)
            with eng.Fori(2, SEQS) as s:
                g(s, s - 1, s - 2)
            l(0, 0, "G")
            l(0, 1, "G")
            l(0, 2)
            with eng.Fori(3, SEQS) as s:
                l(0, s)
            with eng.Fori(1, DEPTH) as layer:
                l(layer, 0)
                l(layer, 1)
                l(layer, 2)
                with eng.Fori(3, SEQS) as s:
                    l(layer, s)
            n = SEQS * DEPTH

            def last(seq):
                return Stage("L", seq, DEPTH - 1)
            body(Body(None, last(SEQS - 1), last(SEQS - 2), last(SEQS - 3),
                      SEQS + n, SEQS + n - 1, n - 2, n - 3, 2 * SEQS + n - 2))
            body(Body(None, None, last(SEQS - 1), last(SEQS - 2), SEQS + n, SEQS + n, n - 1, n - 2, 2 * SEQS + n - 1))
            body(Body(None, None, None, last(SEQS - 1), SEQS + n, SEQS + n, n, n - 1, 2 * SEQS + n))

        def sequences(eng, step):
            step(0)
            with eng.Fori(1, SEQS) as s:
                step(s)

        @block.sync
        def _(sp):
            sp.dma_start(idx[:, :], ids).then_inc(s_ids, 16)
            consts = [(tab, tab_g), (tabB, tab_l), (idb, eye16), (idf, eye32), (mk, masks), (par, l_par), (bO, bo)]
            sp.dma_start(bQKV[:, :], bqkv).then_inc(s_const, 16)
            for dst, src in consts:
                sp.dma_start(dst[:], src).then_inc(s_const, 16)
            sp.dma_start(qks[:].rearrange("p l k d -> p (l k d)"), l_qk_scale.to_broadcast((P, DEPTH * 2 * DH))).then_inc(s_const, 16)

            def load_wo(src):
                sp.dma_start(Wo[:, :, :], src.rearrange("(a p) m -> p a m", p=P)).then_inc(w_o, 16)

            def load_w1(layer):
                sp.dma_start(W1raw[:, :, :], l_w1[layer].rearrange("(k p) n -> p k n", p=P)).then_inc(w_1, 16)

            def load_w2(layer):
                w2 = l_w2[layer]
                sp.dma_start(W2[:, 0:MT - 1, :], w2[0:(MT - 1) * P, :].rearrange("(m p) n -> p m n", p=P)).then_inc(w_2, 16)
                sp.dma_start(W2[0:MLAST, MT - 1, :], w2[(MT - 1) * P:HID, :]).then_inc(w_2, 16)

            def load_qkv(layer):
                for half in range(2):
                    for kind in range(3):
                        last = max(c for c, (k_, _, h_) in enumerate(CHUNKS) if (k_, h_) == (kind, half))
                        sp.wait_ge(pe_q, least(NCH * (SEQS * (layer + 1) - 1) + last + 1))
                        at = kind * INNER + half * HALF
                        for k in range(KD):
                            sp.dma_start(Wraw[:, k, kind, half * HALF:(half + 1) * HALF],
                                         l_wqkv[layer, k * P:(k + 1) * P, at:at + HALF]).then_inc(w_q[3 * half + kind], 16)

            def keep(s):
                sp.wait_ge(v_res, s + 1)
                sp.dma_start(kept[:, :, s:s + 1, :], hT[:, :, s:s + 1, :]).then_inc(s_keep, 16)

            for half in range(2):
                for kind, src in enumerate((wq, wk, wv)):
                    for k in range(KD):
                        sp.dma_start(Wraw[:, k, kind, half * HALF:(half + 1) * HALF].rearrange("p (h d) -> p h d", d=DH),
                                     src[half * 8:half * 8 + 8, k * P:(k + 1) * P, :].rearrange("h p d -> p h d")
                                     ).then_inc(w_q[3 * half + kind], 16)
            load_wo(wo)
            sp.wait_ge(v_em, SEQS)
            load_w2(0)
            for s in range(SEQS - 2):
                keep(s)
            load_qkv(0)
            keep(SEQS - 2)
            keep(SEQS - 1)
            sp.wait_ge(pe_wo, SEQS)
            load_wo(l_wo[0])
            sp.wait_ge(v_xf, SEQS)
            sp.wait_ge(s_keep, 16 * SEQS)
            load_w1(0)
            with sp.Fori(1, DEPTH) as layer:
                load_qkv(layer)
                sp.wait_ge(pe_wo, SEQS * (layer + 1))
                load_wo(l_wo[layer])
                sp.wait_ge(pe_w1, 6 * SEQS * layer)
                load_w1(layer)
                sp.wait_ge(pe_w2, SEQS * layer)
                load_w2(layer)
            sp.wait_ge(pe_tk, UNITS * SEQS * (DEPTH + 1))
            sp.dma_start(hb[:, :, :, :], kept).then_inc(s_hb, 16)
            def store(s):
                sp.wait_ge(a_y, s + 1)
                sp.dma_start(out[s].rearrange("(t p) c -> p t c", p=P), yo[:, :, :]).then_inc(s_out, 16)
            sequences(sp, store)
            sp.wait_ge(s_out, 16 * SEQS)

        N_CONST = 16 * 9

        @block.tensor
        def _(pe):
            mm = nc.tensor.matmul
            held = {}

            def take(bank, *read):
                for s, value in held[bank.name]:
                    pe.wait_ge(s, value)
                held[bank.name] = [read]
                return bank

            def project(b, c):
                kind, t, half = CHUNKS[c]
                ps = take(A[c % 2], a_q, NCH * b.n_q + c + 1)
                if c == 0:
                    pe.wait_ge(v_xs, 2 * (b.n_q + 1))
                layer = 0 if b.q.kind == "G" else b.q.layer + 1
                if t == 0:
                    pe.wait_ge(v_wl, 6 * layer + 3 * half + kind + 1)
                cols = slice(half * HALF, (half + 1) * HALF)
                toks = slice(t * P, (t + 1) * P)
                if b.q.kind == "G":
                    row = 2 * kind + half
                    mm(ps[:, :], idf[0:6, row:row + 1].to_broadcast((6, P)), bQKV[:, :], start=True, stop=False)
                for k in range(KD):
                    mm(ps[:, :], xsh[:, k, toks], Wh[:, k, kind, cols], start=(k == 0 and b.q.kind == "L"), stop=False)
                    mm(ps[:, :], xsh[:, k, toks], Wl[:, k, kind, cols], start=False, stop=False)
                    last = mm(ps[:, :], xsl[:, k, toks], Wh[:, k, kind, cols], start=False, stop=(k == KD - 1))
                last.then_inc(pe_q, 1)

            def turn_qk(b, u):
                half = u // 2
                n_before = b.n_a + 1
                n = UNITS * b.n_a + u + 1
                if u % 2 == 0 and b.a.kind == "G":
                    pe.wait_ge(g_add, least(8 * n_before - (4 if half == 0 else 0)))
                elif u % 2 == 0:
                    pe.wait_ge(g_rot, least(8 * (n_before - SEQS) - (4 if half == 0 else 0)))
                for kind, done, read in ((0, pe_tq, a_qT), (1, pe_tk, v_kT)):
                    ps = take(T[kind], read, n)
                    for a in range(2):
                        pair = 2 * u + a
                        for t in range(TT):
                            last = nc.tensor.transpose(ps[:, a * SEQ + t * P:a * SEQ + (t + 1) * P],
                                                       qr[:, t, kind, pair * P:(pair + 1) * P], idf[:, :])
                    last.then_inc(done, 1)

            def scores(b, u):
                n = UNITS * b.n_a + u
                causal = b.a.kind == "G"
                m0 = 0 if causal else P + SEQ
                w1 = SEQ if causal else SEQ - WINDOW
                pe.wait_ge(a_qT, n + 1)
                pe.wait_ge(v_kT, n + 1)
                pe.wait_ge(a_x0, n)
                mm(S0[:, :], idb[:, :], mk[:, None, m0:m0 + P].to_broadcast((P, 4, P)), start=True, stop=False)
                for a in range(2):
                    last = mm(S0[:, a * SEQ:(a + 1) * SEQ], qT[:, u % 2, a, 0:P], kT[:, u % 2, a, :, 0:P],
                              start=False, stop=(a == 1))
                last.then_inc(pe_s0, 1)
                pe.wait_ge(a_x1, n)
                for a in range(2):
                    mm(S1[:, a, 0:2 * w1], idb[:, :], mk[:, None, m0 + P:m0 + P + w1].to_broadcast((P, 2, w1)),
                       start=True, stop=False)
                    last = mm(S1[:, a, 0:2 * w1], qT[:, u % 2, a, P:SEQ], kT[:, u % 2, a, :, SEQ - w1:SEQ],
                              start=False, stop=True)
                last.then_inc(pe_s1, 1)

            def turn_p(b, u, pair):
                rows = P if b.a.kind == "G" else WINDOW
                for h in (2 * pair, 2 * pair + 1):
                    pe.wait_ge(g_p, 16 * b.n_a + 4 * u + h + 1)
                    ps = take(T[h % 2], a_pt, 16 * b.n_a + 4 * u + h + 1)
                    nc.tensor.transpose(ps[:, 0:P], Pr[:, 1, h, P:SEQ], idf[:, :])
                    nc.tensor.transpose(ps[:, P:2 * P], Pr[:, 0, h, 0:P], idf[:, :])
                    nc.tensor.transpose(ps[:, 2 * P:2 * P + rows], Pr[0:rows, 1, h, 0:P], idf[0:rows, 0:rows]
                                        ).then_inc(pe_pt, 1)

            def values(b, u):
                pe.wait_ge(v_ot, UNITS * b.n_a + u)
                if u == 0 and b.f:
                    pe.wait_ge(v_ln, N_LN * (b.n_ln + 1))
                for h in range(4):
                    a, e = h // 2, h % 2
                    cols = slice((4 * u + h) * DH, (4 * u + h + 1) * DH)
                    pe.wait_ge(a_pt, 16 * b.n_a + 4 * u + h + 1)
                    mm(O[e * DH:(e + 1) * DH, a * SEQ:(a + 1) * SEQ], V[:, 0, cols], PT[:, h, P:P + SEQ],
                       start=True, stop=False)
                    last = mm(O[e * DH:(e + 1) * DH, a * SEQ + P:(a + 1) * SEQ], V[:, 1, cols], PT[:, h, 0:P],
                              start=False, stop=True)
                last.then_inc(pe_o, 1)

            def out_project(b):
                layer = 0 if b.a.kind == "G" else b.a.layer + 1
                ps = take(A[0], v_res, b.n_a + 1)
                pe.wait_ge(w_o, 16 * (layer + 1))
                pe.wait_ge(v_ot, UNITS * (b.n_a + 1))
                for m in range(KD):
                    for a in range(PAIRS):
                        last = mm(ps[:, m * SEQ:(m + 1) * SEQ], Wo[:, a, m * P:(m + 1) * P], OT[:, a, :],
                                  start=(a == 0), stop=(a == PAIRS - 1))
                last.then_inc(pe_wo, 1)

            def ln_mean(b, ready):
                ps = take(A[0], v_ln, N_LN * b.n_ln + 1)
                pe.wait_ge(*ready)
                for k in range(KD):
                    last = mm(ps[:, 0:SEQ], onesN[:, :], xf[:, k, :], start=(k == 0), stop=(k == KD - 1))
                last.then_inc(pe_ln, 1)

            def ln_var(b):
                ps = take(A[1], v_ln, N_LN * b.n_ln + 2)
                pe.wait_ge(a_sq, b.n_ln + 1)
                for k in range(KD):
                    last = mm(ps[:, 0:SEQ], onesN[:, :], sqF[:, k, :], start=(k == 0), stop=(k == KD - 1))
                last.then_inc(pe_ln, 1)

            def ln_turn(b):
                pe.wait_ge(v_ot, UNITS * b.n_a)
                pe.wait_ge(v_ln, N_LN * b.n_ln + 2)
                for t in range(TT):
                    last = nc.tensor.transpose(O[:, t * P:(t + 1) * P], vr[:, t * P:(t + 1) * P], idf[:, :])
                last.then_inc(pe_ln, 1)

            def ln_spread(b):
                pe.wait_ge(v_ln, N_LN * b.n_ln + 2 + N_NEWTON)
                for t in range(TT):
                    last = nc.tensor.transpose(O[:, SEQ + t * P:SEQ + (t + 1) * P], ry[:, t:t + 1].to_broadcast((P, P)),
                                               idf[:, :])
                last.then_inc(pe_ln, 1)

            def up(b, slot):
                ps = take(A[UP_BANK[slot]], *((a_gelu, 3 * b.n_f + slot + 1) if slot < 3 else (v_hid, 3 * b.n_f + slot - 2)))
                if slot == 0:
                    pe.wait_ge(v_w1l, b.f.layer + 1)
                    pe.wait_ge(v_xn, b.n_ln + 1)
                base = HID if slot < 3 else 0
                for m in (2 * (slot % 3), 2 * (slot % 3) + 1):
                    n = P if m < MT - 1 else MLAST
                    to, cols = ps[0:n, (m % 2) * SEQ:(m % 2 + 1) * SEQ], slice(base + m * P, base + m * P + n)
                    for k in range(KD):
                        mm(to, W1h[:, k, cols], xnh[:, k, :], start=(k == 0), stop=False)
                        mm(to, W1h[:, k, cols], xnl[:, k, :], start=False, stop=False)
                        last = mm(to, W1l[:, k, cols], xnh[:, k, :], start=False, stop=(k == KD - 1))
                last.then_inc(pe_w1, 1)

            def down(b, o):
                if o == 0:
                    take(A[1], v_out, b.n_d + 1)
                    pe.wait_ge(w_2, 32 * (b.d.layer + 1))
                    pe.wait_ge(v_hid, 3 * (b.n_d + 1))
                for m in range(MT):
                    n = P if m < MT - 1 else MLAST
                    last = mm(A[1][:, o * SEQ:(o + 1) * SEQ], W2[0:n, m, o * P:(o + 1) * P], G[0:n, m, :],
                              start=(m == 0), stop=(m == MT - 1))
                if o == KD - 1:
                    last.then_inc(pe_w2, 1)

            def body(b):
                held["A1"] = [(a_q, NCH * b.n_q), (v_ln, N_LN * b.n_ln - (N_LN - 2))]
                held["A0"] = held["A1"] + [(v_res, b.n_a)]
                held["T0"] = held["T1"] = [(a_pt, 16 * b.n_a)]
                ffn = b.f is not None and b.f.kind == "L"
                if b.a:
                    if b.a.kind == "L" and isinstance(b.n_a, int) and b.n_a == SEQS:
                        pe.wait_ge(pad_ready, 2)
                    turn_qk(b, 0)
                if b.d:
                    down(b, 0)
                if b.a:
                    turn_qk(b, 1)
                if b.d:
                    down(b, 1)
                if b.f:
                    ln_mean(b, (v_xf, b.n_ln - SEQS + 1))
                if b.a:
                    scores(b, 0)
                if b.f:
                    ln_var(b)
                if b.q:
                    project(b, 0)
                if b.f:
                    ln_turn(b)
                if b.q:
                    project(b, 1)
                    project(b, 2)
                if b.f:
                    ln_spread(b)
                if b.a:
                    turn_p(b, 0, 0)
                if b.q:
                    project(b, 3)
                if b.a:
                    turn_p(b, 0, 1)
                    scores(b, 1)
                    values(b, 0)
                if ffn:
                    up(b, 0)
                if b.a:
                    turn_qk(b, 2)
                if ffn:
                    up(b, 1)
                if b.a:
                    turn_p(b, 1, 0)
                if ffn:
                    up(b, 2)
                if b.a:
                    turn_p(b, 1, 1)
                    scores(b, 2)
                    values(b, 1)
                if ffn:
                    up(b, 3)
                if b.q:
                    project(b, 4)
                    project(b, 5)
                if b.a:
                    turn_qk(b, 3)
                if b.q:
                    project(b, 6)
                if b.a:
                    turn_p(b, 2, 0)
                if ffn:
                    up(b, 4)
                if b.a:
                    turn_p(b, 2, 1)
                    scores(b, 3)
                    values(b, 2)
                if b.q:
                    project(b, 7)
                    project(b, 8)
                if b.a:
                    turn_p(b, 3, 0)
                if b.q:
                    project(b, 9)
                if b.a:
                    turn_p(b, 3, 1)
                if b.q:
                    project(b, 10)
                if ffn:
                    up(b, 5)
                if b.a:
                    values(b, 3)
                if b.q:
                    project(b, 11)
                if b.a:
                    out_project(b)

            pe.wait_ge(s_const, N_CONST)
            pe.wait_ge(zeroed, 5)
            def embed(s):
                pe.wait_ge(v_em, s + 1)
                pe.wait_ge(a_e, s)
                for k in range(KD):
                    for t in range(TT):
                        last = nc.tensor.transpose(T[0][:, k * SEQ + t * P:k * SEQ + (t + 1) * P],
                                                   em[:, t, k * P:(k + 1) * P], idf[:, :])
                last.then_inc(pe_e, 1)
                held["A0"] = held["A1"] = [(v_ln, N_LN * s)]
                b = Body(None, None, None, None, 0, 0, 0, 0, s)
                ln_mean(b, (a_e, s + 1))
                ln_var(b)
                ln_turn(b)
                ln_spread(b)
            sequences(pe, embed)
            pe.wait_ge(v_ln, N_LN * SEQS)
            bodies(pe, body)
            def restore(s):
                pe.wait_ge(v_y, s + 1)
                pe.wait_ge(a_y, s)
                for t in range(TT):
                    for k in range(KD):
                        last = nc.tensor.transpose(T[0][:, t * DIM + k * P:t * DIM + (k + 1) * P],
                                                   yb[:, k, t * P:(t + 1) * P], idf[:, :])
                last.then_inc(pe_y, 1)
            sequences(pe, restore)

        @block.scalar
        def _(act):
            f = nc.scalar.activation

            def evac_chunk(b, c):
                kind, t, half = CHUNKS[c]
                ps = A[c % 2]
                act.wait_ge(pe_q, NCH * b.n_q + c + 1)
                if kind == 2:
                    act.wait_ge(pe_o, UNITS * b.n_a + (2 * (half + 1) if b.a else 0))
                    f(V[:, t, half * HALF:(half + 1) * HALF], ps[:, :], ACT.Copy).then_inc(a_q, 1)
                    return
                slot = QK_SLOT.index(c)
                act.wait_ge(v_rot, least(8 * b.n_q + slot - 1))
                if b.q.kind == "L":
                    f(sq[:, slot % 2, :], ps[:, :], ACT.Square)
                f(raw[:, slot % 2, :], ps[:, :], ACT.Copy).then_inc(a_q, 1)

            def cut_qkv(b, half):
                layer = 0 if b.q.kind == "G" else b.q.layer + 1
                for kind in range(3):
                    act.wait_ge(w_q[3 * half + kind], 32 * (layer + 1))
                    f(Wh[:, :, kind, half * HALF:(half + 1) * HALF],
                      Wraw[:, :, kind, half * HALF:(half + 1) * HALF], ACT.Copy).then_inc(a_wh, 1)

            def cut_w1(b):
                act.wait_ge(w_1, 16 * (b.q.layer + 1))
                f(W1h[:, :, :], W1raw[:, :, :], ACT.Copy).then_inc(a_w1h, 1)

            def evac_q(b, u):
                n = UNITS * b.n_a + u
                act.wait_ge(pe_tq, n + 1)
                act.wait_ge(pe_s1, least(n - 1))
                f(qT[:, u % 2, :, :], T[0][:, :].rearrange("p (a q) -> p a q", a=2), ACT.Copy).then_inc(a_qT, 1)

            def exps(b, u):
                n = UNITS * b.n_a + u
                w1 = SEQ if b.a.kind == "G" else SEQ - WINDOW
                act.wait_ge(pe_pt, 4 * n)
                act.wait_ge(v_max, 2 * n + 1)
                for h in range(4):
                    last = f(Pr[:, 0, h, 0:P], S0[:, h * P:(h + 1) * P], ACT.Exp, bias=nm[:, u % 2, h:h + 1],
                             accum_out=rs[:, u % 2, h:h + 1])
                last.then_inc(a_x0, 1)
                act.wait_ge(v_max, 2 * n + 2)
                for h in range(4):
                    last = f(Pr[:, 1, h, SEQ - w1:SEQ], S1[:, h // 2, (h % 2) * w1:(h % 2 + 1) * w1], ACT.Exp,
                             bias=nm[:, u % 2, 4 + h:5 + h], accum_out=rs[:, u % 2, 4 + h:5 + h])
                last.then_inc(a_x1, 1)

            def evac_p(b, u, pair):
                width = P + SEQ if b.a.kind == "G" else 2 * P + WINDOW
                for h in (2 * pair, 2 * pair + 1):
                    act.wait_ge(pe_pt, 16 * b.n_a + 4 * u + h + 1)
                    act.wait_ge(pe_o, UNITS * b.n_a + u)
                    f(PT[:, h, 0:width], T[h % 2][:, 0:width], ACT.Copy).then_inc(a_pt, 1)

            def squares(b):
                act.wait_ge(v_ln, N_LN * b.n_ln + 1)
                act.wait_ge(pe_ln, 4 * b.n_ln)
                f(sqF[:, :, :], xc[:, :, :], ACT.Square).then_inc(a_sq, 1)

            def gelus(b, slot):
                act.wait_ge(pe_w1, 6 * b.n_f + slot + 1)
                act.wait_ge(pe_w2, b.n_f)
                act.wait_ge(v_bG, b.n_f + 1)
                for m in (2 * slot, 2 * slot + 1):
                    n = P if m < MT - 1 else MLAST
                    last = f(G[0:n, m, :], A[UP_BANK[slot]][0:n, (m % 2) * SEQ:(m % 2 + 1) * SEQ], ACT.Gelu,
                             bias=bG[0:n, m:m + 1])
                last.then_inc(a_gelu, 1)

            def body(b):
                ffn = b.f is not None and b.f.kind == "L"
                first = b.q is not None and isinstance(b.q.seq, int) and b.q.seq == 0
                second = b.q is not None and b.q.kind == "L" and isinstance(b.q.seq, int) and b.q.seq == 1
                if b.a:
                    evac_q(b, 0)
                    evac_q(b, 1)
                if b.f:
                    squares(b)
                if first:
                    cut_qkv(b, 0)
                if b.a:
                    exps(b, 0)
                if b.q:
                    evac_chunk(b, 0)
                    evac_chunk(b, 1)
                    evac_chunk(b, 2)
                if b.a:
                    evac_p(b, 0, 0)
                    evac_p(b, 0, 1)
                    exps(b, 1)
                if b.q:
                    evac_chunk(b, 3)
                if b.a:
                    evac_q(b, 2)
                if first:
                    cut_qkv(b, 1)
                if ffn:
                    gelus(b, 0)
                    gelus(b, 1)
                if b.a:
                    evac_p(b, 1, 0)
                if ffn:
                    gelus(b, 2)
                if b.a:
                    evac_p(b, 1, 1)
                    exps(b, 2)
                if b.q:
                    evac_chunk(b, 4)
                    evac_chunk(b, 5)
                if b.a:
                    evac_q(b, 3)
                if b.q:
                    evac_chunk(b, 6)
                if b.a:
                    evac_p(b, 2, 0)
                    evac_p(b, 2, 1)
                    exps(b, 3)
                if b.q:
                    evac_chunk(b, 7)
                    evac_chunk(b, 8)
                if b.a:
                    evac_p(b, 3, 0)
                if b.q:
                    evac_chunk(b, 9)
                if b.a:
                    evac_p(b, 3, 1)
                if b.q:
                    evac_chunk(b, 10)
                    evac_chunk(b, 11)
                if second:
                    cut_w1(b)

            act.wait_ge(s_const, N_CONST)
            def embed(s):
                act.wait_ge(pe_e, s + 1)
                ps = T[0][:, :].rearrange("p (k q) -> p k q", k=KD)
                act.wait_ge(pe_ln, 4 * s)
                act.wait_ge(v_ln, N_LN * s)
                f(xf[:, :, :], ps, ACT.Copy)
                f(hT[:, :, ds(s, 1), :], ps[:, :, None, :], ACT.Copy).then_inc(a_e, 1)
                squares(Body(None, None, None, None, 0, 0, 0, 0, s))
            sequences(act, embed)
            bodies(act, body)
            def restore(s):
                act.wait_ge(pe_y, s + 1)
                act.wait_ge(s_out, 16 * s)
                f(yo[:, :, :], T[0][:, :].rearrange("p (t c) -> p t c", t=TT), ACT.Copy).then_inc(a_y, 1)
            sequences(act, restore)

        @block.vector
        def _(dve):
            v = nc.vector
            MAGIC = float(0x5F3759DF)

            def chain(s, base):
                n = [0]

                def link(ins):
                    n[0] += 1
                    ins.then_inc(s, 1)
                    dve.wait_ge(s, base + n[0])
                return link

            def newton(x, y, t, link):
                link(v.tensor_scalar(t.bitcast(i32), x.bitcast(i32), 1, None, ALU.logical_shift_right))
                link(v.tensor_scalar(y.bitcast(i32), t.bitcast(i32), -1.0, MAGIC, ALU.mult, ALU.add))
                for i in range(3):
                    link(v.scalar_tensor_tensor(t, y, -0.5, y, ALU.mult, ALU.mult))
                    link(v.tensor_tensor(t, t, x, ALU.mult))
                    last = v.scalar_tensor_tensor(y, t, 1.5, y, ALU.add, ALU.mult)
                    if i < 2:
                        link(last)
                return last

            def copy(to, of):
                return v.tensor_scalar(to, of, 1.0, None, ALU.mult)

            def take_input(b):
                s = b.q.seq
                dve.wait_ge(pe_q, NCH * b.n_q)
                if b.q.kind == "G":
                    x = xT[:, :, ds(s, 1), 1:SEQ + 1]
                    copy(xsh[:, :, None, :], x).then_inc(v_xs, 1)
                    dve.wait_ge(v_xs, 2 * b.n_q + 1)
                    v.tensor_tensor(xsl[:, :, None, :], x, xsh[:, :, None, :].bitcast(f32), ALU.subtract).then_inc(v_xs, 1)
                    return
                if isinstance(b.q.layer, int):
                    dve.wait_ge(v_xn, SEQS + s + 1)
                else:
                    dve.wait_ge(v_out, least(b.n_q - 2 * SEQS + 1))
                x = xT[:, 0, ds(s, 1), 1:SEQ + 1], xT[:, 1, ds(s, 1), 0:SEQ]
                for k in range(KD):
                    last = copy(xsh[:, k, None, :], x[k])
                last.then_inc(v_xs, 1)
                dve.wait_ge(v_xs, 2 * b.n_q + 1)
                for k in range(KD):
                    last = v.tensor_tensor(xsl[:, k, None, :], x[k], xsh[:, k, None, :].bitcast(f32), ALU.subtract)
                last.then_inc(v_xs, 1)

            def cut_qkv(b, half):
                layer = 0 if b.q.kind == "G" else b.q.layer + 1
                for kind in range(3):
                    cols = slice(half * HALF, (half + 1) * HALF)
                    dve.wait_ge(a_wh, 6 * layer + 3 * half + kind + 1)
                    v.tensor_tensor(Wl[:, :, kind, cols], Wraw[:, :, kind, cols],
                                    Wh[:, :, kind, cols].bitcast(f32), ALU.subtract).then_inc(v_wl, 1)

            def cut_w1(b):
                dve.wait_ge(a_w1h, b.q.layer + 1)
                v.tensor_tensor(W1l[:, :, :], W1raw[:, :, :], W1h[:, :, :].bitcast(f32),
                                ALU.subtract).then_inc(v_w1l, 1)

            def layer_tables(b):
                L = ds(b.q.layer, 1)
                dve.wait_ge(v_rot, 8 * b.n_q)
                for kind in range(2):
                    c, sn = 2 * kind, 2 * kind + 1
                    w = qks[:, L, kind, :].to_broadcast((P, TT, DH))
                    v.tensor_tensor(tab[:, :, c, :], tabB[:, :, c, :], w, ALU.mult)
                    for x in range(2):
                        to, of = slice(32 * x, 32 * x + 32), slice(32 - 32 * x, 64 - 32 * x)
                        w = qks[:, L, kind, of].to_broadcast((P, TT, 32))
                        last = v.tensor_tensor(tab[:, :, sn, to], tabB[:, :, sn, to], w, ALU.mult)
                last.then_inc(v_tab, 1)
                dve.wait_ge(v_tab, b.q.layer + 1)

            def gate_biases(b):
                dve.wait_ge(a_gelu, 3 * b.n_f)
                copy(bG[:, None, :], par[:, ds(b.f.layer, 1), 10:10 + MT]).then_inc(v_bG, 1)

            def copy_f(b):
                s = b.f.seq
                dve.wait_ge(pe_ln, 4 * b.n_ln)
                dve.wait_ge(v_res, least(b.n_ln - SEQS + 1))
                if b.f.kind == "G":
                    copy(xf[:, :, None, :], hT[:, :, ds(s, 1), :]).then_inc(v_xf, 1)
                else:
                    copy(xf[:, 0, None, :], xT[:, 0, ds(s, 1), 1:SEQ + 1])
                    copy(xf[:, 1, None, :], xT[:, 1, ds(s, 1), 0:SEQ]).then_inc(v_xf, 1)

            def evac_k(b, u):
                n = UNITS * b.n_a + u
                dve.wait_ge(pe_tk, n + 1)
                dve.wait_ge(pe_s1, least(n - 1))
                for e in range(2):
                    rows = slice(e * DH, (e + 1) * DH)
                    last = v.tensor_copy(kT[rows, u % 2, :, e, :], T[1][rows, :].rearrange("p (a q) -> p a q", a=2))
                last.then_inc(v_kT, 1)

            def maxima(b, u):
                n = UNITS * b.n_a + u
                w1 = SEQ if b.a.kind == "G" else SEQ - WINDOW
                dve.wait_ge(pe_s0, n + 1)
                v.tensor_reduce(nm[:, u % 2, 0:4], S0[:, :].rearrange("p (h k) -> p h k", h=4), axis=AX.X,
                                op=ALU.max, negate=True).then_inc(v_max, 1)
                dve.wait_ge(pe_s1, n + 1)
                v.tensor_reduce(nm[:, u % 2, 4:8], S1[:, :, 0:2 * w1].rearrange("p a (h k) -> p a h k", h=2),
                                axis=AX.X, op=ALU.max, negate=True).then_inc(v_max, 1)

            def reciprocals(b, u):
                n = UNITS * b.n_a + u
                dve.wait_ge(a_x1, n + 1)
                v.reciprocal(rr[:, u % 2, :], rs[:, u % 2, :]).then_inc(v_rec, 1)

            def rotate(b, slot):
                c = QK_SLOT[slot]
                kind, t, half = CHUNKS[c]
                dve.wait_ge(a_q, NCH * b.n_q + c + 1)
                if b.q.kind == "L":
                    i = slot % 4
                    v.tensor_reduce(ssq[:, i * 8:(i + 1) * 8], sq[:, slot % 2, :].rearrange("p (h d) -> p h d", d=DH),
                                    axis=AX.X, op=ALU.add)
                dve.wait_ge(pe_tk, UNITS * b.n_a + (2 * (half + 1) if b.a else 0))
                r = raw[:, slot % 2, :]
                v.tensor_tensor(qr[:, t, kind, half * HALF:(half + 1) * HALF].rearrange("p (h d) -> p h d", d=DH),
                                r.rearrange("p (h d) -> p h d", d=DH),
                                tab[:, t, 2 * kind, :][:, None, :].to_broadcast((P, 8, DH)), ALU.mult)
                dve.wait_ge(g_add, least(8 * b.n_q + slot - 1))
                v.tensor_tensor(t2[:, slot % 2, :].rearrange("p (h x d) -> p h x d", x=2, d=32),
                                r.rearrange("p (h x d) -> p h x d", x=2, d=32)[:, :, ::-1, :],
                                tab[:, t, 2 * kind + 1, :].rearrange("p (x d) -> p x d", x=2)[:, None, :, :]
                                .to_broadcast((P, 8, 2, 32)), ALU.mult).then_inc(v_rot, 1)

            def norms(b, half):
                if b.q.kind == "G":
                    return
                n = 2 * (b.n_q - SEQS) + half
                link = chain(v_nrm, N_NEWTON * n)
                dve.wait_ge(v_rot, 8 * b.n_q + 4 * half + 4)
                dve.wait_ge(g_rot, 4 * n)
                link(v.tensor_scalar(ssq[:, :], ssq[:, :], 1e-24, None, ALU.max))
                newton(ssq[:, :], rn[:, :], nt[:, :], link).then_inc(v_rn, 1)

            def centre(b):
                n = b.n_ln
                dve.wait_ge(pe_ln, 4 * n + 1)
                dve.wait_ge(a_sq, n)
                v.tensor_tensor(xc[:, :, :], xf[:, :, :], A[0][:, None, 0:SEQ].to_broadcast((P, KD, SEQ)),
                                ALU.subtract).then_inc(v_ln, 1)

            def variance(b):
                dve.wait_ge(pe_ln, 4 * b.n_ln + 2)
                v.tensor_scalar(vr[:, :], A[1][:, 0:SEQ], 1e-5, None, ALU.add).then_inc(v_ln, 1)

            def root(b):
                dve.wait_ge(pe_ln, 4 * b.n_ln + 3)
                newton(O[:, 0:SEQ:P], ry[:, :], rt[:, :], chain(v_ln, N_LN * b.n_ln + 2)).then_inc(v_ln, 1)

            def normalise(b):
                n = b.n_ln
                dve.wait_ge(pe_ln, 4 * n + 4)
                v.tensor_tensor(xc[:, :, :], xc[:, :, :], O[:, None, SEQ:2 * SEQ].to_broadcast((P, KD, SEQ)),
                                ALU.mult).then_inc(v_ln, 1)
                dve.wait_ge(v_ln, N_LN * (n + 1))
                if b.f.kind == "G":
                    copy(xT[:, :, ds(b.f.seq, 1), 1:SEQ + 1], xc[:, :, None, :]).then_inc(v_xn, 1)
                    return
                for k in range(KD):
                    last = v.tensor_scalar(xc[:, k, :], xc[:, k, :], par[:, ds(b.f.layer, 1), k],
                                           par[:, ds(b.f.layer, 1), 2 + k], ALU.mult, ALU.add)
                last.then_inc(v_aff, 1)
                dve.wait_ge(v_aff, 2 * b.n_f + 1)
                dve.wait_ge(pe_w1, 6 * b.n_f)
                copy(xnh[:, :, :], xc[:, :, :]).then_inc(v_aff, 1)
                dve.wait_ge(v_aff, 2 * b.n_f + 2)
                v.tensor_tensor(xnl[:, :, :], xc[:, :, :], xnh[:, :, :].bitcast(f32), ALU.subtract).then_inc(v_xn, 1)

            def evac_o(b, u):
                n = UNITS * b.n_a + u
                dve.wait_ge(pe_o, n + 1)
                dve.wait_ge(pe_wo, b.n_a)
                v.tensor_copy(OT[:, 2 * u:2 * u + 2, :], O[:, :].rearrange("p (a q) -> p a q", a=2)).then_inc(v_ot, 1)

            def hidden(b, slot):
                dve.wait_ge(pe_w1, 6 * b.n_f + slot + 1)
                dve.wait_ge(a_gelu, 3 * b.n_f + slot - 2)
                for m in (2 * (slot - 3), 2 * (slot - 3) + 1):
                    n = P if m < MT - 1 else MLAST
                    last = v.scalar_tensor_tensor(
                        G[0:n, m, :], A[UP_BANK[slot]][0:n, (m % 2) * SEQ:(m % 2 + 1) * SEQ],
                        par[0:n, ds(b.f.layer, 1), 4 + m], G[0:n, m, :], ALU.add, ALU.mult)
                last.then_inc(v_hid, 1)

            def add_attention(b):
                dve.wait_ge(pe_wo, b.n_a + 1)
                s = b.a.seq
                if b.a.kind == "G":
                    for k in range(KD):
                        h = hT[:, k, ds(s, 1), :]
                        last = v.scalar_tensor_tensor(h, A[0][:, None, k * SEQ:(k + 1) * SEQ], bO[:, k:k + 1], h,
                                                      ALU.add, ALU.add)
                else:
                    x = xT[:, :, ds(s, 1), 1:SEQ + 1]
                    last = v.tensor_tensor(x, x, A[0][:, :].rearrange("p (k o q) -> p k o q", k=KD, o=1), ALU.add)
                last.then_inc(v_res, 1)

            def add_ffn(b):
                dve.wait_ge(pe_w2, b.n_d + 1)
                for k in range(KD):
                    x = xT[:, k, ds(b.d.seq, 1), 1:SEQ + 1]
                    last = v.scalar_tensor_tensor(x, A[1][:, None, k * SEQ:(k + 1) * SEQ],
                                                  par[:, ds(b.d.layer, 1), 16 + k], x, ALU.add, ALU.add)
                last.then_inc(v_out, 1)

            def body(b):
                ffn = b.f is not None and b.f.kind == "L"
                first = b.q is not None and isinstance(b.q.seq, int) and b.q.seq == 0
                second = b.q is not None and b.q.kind == "L" and isinstance(b.q.seq, int) and b.q.seq == 1
                if b.q and b.q.kind == "L" and isinstance(b.q.seq, int) and b.q.seq == 0:
                    layer_tables(b)
                if b.a:
                    evac_k(b, 0)
                if b.f:
                    copy_f(b)
                if b.q:
                    take_input(b)
                if b.a:
                    evac_k(b, 1)
                if ffn:
                    gate_biases(b)
                if b.f:
                    centre(b)
                if b.d:
                    add_ffn(b)
                if first:
                    cut_qkv(b, 0)
                if b.a:
                    maxima(b, 0)
                if b.f:
                    variance(b)
                if b.a:
                    reciprocals(b, 0)
                if b.f:
                    root(b)
                if b.q:
                    rotate(b, 0)
                if b.f:
                    normalise(b)
                if b.a:
                    maxima(b, 1)
                if b.q:
                    rotate(b, 1)
                if b.a:
                    evac_o(b, 0)
                    reciprocals(b, 1)
                if b.q:
                    rotate(b, 2)
                if b.a:
                    evac_k(b, 2)
                if b.q:
                    rotate(b, 3)
                if first:
                    cut_qkv(b, 1)
                if b.q:
                    norms(b, 0)
                if b.a:
                    maxima(b, 2)
                    evac_o(b, 1)
                if ffn:
                    hidden(b, 3)
                if b.a:
                    reciprocals(b, 2)
                    evac_k(b, 3)
                if b.q:
                    rotate(b, 4)
                if ffn:
                    hidden(b, 4)
                if b.a:
                    maxima(b, 3)
                    evac_o(b, 2)
                    reciprocals(b, 3)
                if b.q:
                    rotate(b, 5)
                    rotate(b, 6)
                if ffn:
                    hidden(b, 5)
                if b.a:
                    evac_o(b, 3)
                if b.q:
                    rotate(b, 7)
                    norms(b, 1)
                if b.a:
                    add_attention(b)
                if second:
                    cut_w1(b)

            v.memset(onesN[:, :], 1.0 / DIM).then_inc(zeroed, 1)
            v.memset(xT[:, :, :, 0:1], 0.0).then_inc(zeroed, 1)
            dve.wait_ge(s_const, N_CONST)
            dve.wait_ge(zeroed, 5)
            dve.wait_ge(s_gat, 16 * 2 * SEQS * TT)
            def embed(s):
                u = gu[:, ds(s * TT, TT), :]
                v.tensor_scalar(u, u, KEEP, float(np.float32(1) / np.float32(KEEP)), ALU.is_lt, ALU.mult).then_inc(v_emb, 1)
                dve.wait_ge(v_emb, s + 1)
                dve.wait_ge(pe_e, s)
                v.tensor_tensor(em[:, :, :], gw[:, ds(s * TT, TT), :], u, ALU.mult).then_inc(v_em, 1)
                b = Body(None, None, Stage("G", s, 0), None, 0, 0, 0, 0, s)
                dve.wait_ge(a_e, s + 1)
                centre(b)
                variance(b)
                root(b)
                normalise(b)
            sequences(dve, embed)
            dve.wait_ge(v_xn, SEQS)
            bodies(dve, body)
            dve.wait_ge(v_out, SEQS * DEPTH)
            dve.wait_ge(s_hb, 16)
            def restore(s):
                dve.wait_ge(pe_y, s)
                v.tensor_tensor(yb[:, :, None, :], hb[:, :, ds(s, 1), :], xT[:, :, ds(s, 1), 1:SEQ + 1],
                                ALU.add).then_inc(v_y, 1)
            sequences(dve, restore)

        @block.gpsimd
        def _(pool):
            p = nc.gpsimd

            def scale_p(b, u):
                w1 = SEQ if b.a.kind == "G" else SEQ - WINDOW
                pool.wait_ge(v_rec, UNITS * b.n_a + u + 1)
                for h in range(4):
                    x, y = Pr[:, 0, h, 0:P], Pr[:, 1, h, SEQ - w1:SEQ]
                    if h == 0:
                        p.tensor_tensor(x, x, rr[:, u % 2, h:h + 1].to_broadcast((P, P)), ALU.mult)
                    else:
                        p.tensor_scalar(x, x, rr[:, u % 2, h:h + 1], 1.0, ALU.mult, ALU.mult)
                    p.tensor_scalar(y, y, rr[:, u % 2, 4 + h:5 + h], 1.0, ALU.mult, ALU.mult).then_inc(g_p, 1)

            def chunk(slot):
                kind, t, half = CHUNKS[QK_SLOT[slot]]
                return qr[:, t, kind, half * HALF:(half + 1) * HALF]

            def add_turned(b, slot):
                pool.wait_ge(v_rot, 8 * b.n_q + slot + 1)
                p.tensor_tensor(chunk(slot), chunk(slot), t2[:, slot % 2, :], ALU.add).then_inc(g_add, 1)

            def scale_qk(b, slots):
                if b.q.kind == "G":
                    return
                for slot in slots:
                    pool.wait_ge(v_rn, 2 * (b.n_q - SEQS) + slot // 4 + 1)
                    i = slot % 4
                    x = chunk(slot).rearrange("p (h d) -> p h d", d=DH)
                    pool.wait_ge(g_add, 8 * b.n_q + slot + 1)
                    p.tensor_tensor(x, x, rn[:, i * 8:(i + 1) * 8, None].to_broadcast((P, 8, DH)),
                                    ALU.mult).then_inc(g_rot, 1)

            def clear_padding(kind):
                if kind == "L":
                    pool.wait_ge(pe_pt, 16 * SEQS)
                    pool.wait_ge(pe_o, UNITS * SEQS)
                done = zeroed if kind == "G" else pad_ready
                p.memset(Pr[:, 1, :, 0:WINDOW], 0.0).then_inc(done, 1)
                p.memset(PT[:, :, 2 * P + WINDOW:P + SEQ], 0.0).then_inc(done, 1)

            def body(b):
                if b.a:
                    if b.a.kind == "L" and isinstance(b.n_a, int) and b.n_a == SEQS:
                        clear_padding("L")
                    scale_p(b, 0)
                if b.q:
                    add_turned(b, 0)
                    add_turned(b, 1)
                if b.a:
                    scale_p(b, 1)
                if b.q:
                    add_turned(b, 2)
                    add_turned(b, 3)
                    scale_qk(b, (0, 1))
                if b.a:
                    scale_p(b, 2)
                if b.q:
                    scale_qk(b, (2, 3))
                    add_turned(b, 4)
                if b.a:
                    scale_p(b, 3)
                if b.q:
                    add_turned(b, 5)
                    add_turned(b, 6)
                    add_turned(b, 7)
                    scale_qk(b, (4, 5, 6, 7))

            p.memset(kT[:, :, :, :, :], 0.0).then_inc(zeroed, 1)
            clear_padding("G")
            pool.wait_ge(s_ids, 16)
            for t in range(SEQS * TT):
                for table, to in ((emb_w, gw), (emb_u, gu)):
                    p.indirect_dma_start(out=to[:, t, :], out_offset=None, in_=table[:, :],
                                         in_offset=bass.IndirectOffsetOnAxis(ap=idx[:, t:t + 1], axis=0)
                                         ).then_inc(s_gat, 16)
            bodies(pool, body)


def kernel(**inputs):
    import concourse.bacc as bacc
    from concourse.bass_utils import run_bass_kernel_spmd

    x = {k: np.ascontiguousarray(a) for k, a in inputs.items()}

    def halves(a, width):
        return a.reshape(DEPTH, -1, width).transpose(2, 0, 1)

    def tiles(a):
        padded = np.zeros((DEPTH, MT * P), a.dtype)
        padded[:, :HID] = a
        return halves(padded, P)

    b1 = x["L0_ffn_b1"]
    params = np.concatenate([halves(x["L0_ffn_ln_g"], P), halves(x["L0_ffn_ln_b"], P), tiles(b1[:, :HID]),
                             tiles(b1[:, HID:]), halves(x["L0_ffn_b2"], P)], 2)
    arrays = {
        "ids": x["x"].reshape(SEQS * TT, P).T,
        "emb_w": x["L0_tok_weight"], "emb_u": x["L0_tok_mask_u"],
        "wq": x["L0_attn_W_Q"], "wk": x["L0_attn_W_K"], "wv": x["L0_attn_W_V"],
        "bqkv": np.concatenate([x[f"L0_attn_b_{n}"].reshape(2, HALF) for n in "QKV"]),
        "wo": x["L0_attn_W_O"].reshape(INNER, DIM), "bo": x["L0_attn_b_O"].reshape(KD, P).T,
        "l_wqkv": x["L0_ffn_Wqkv"],
        "l_qk_scale": np.stack([x["L0_ffn_q_scale"], x["L0_ffn_k_scale"]], 1).reshape(1, -1),
        "l_wo": x["L0_ffn_Wo"], "l_par": params, "l_w1": x["L0_ffn_W1"], "l_w2": x["L0_ffn_W2"],
        **constants(),
    }
    nc = bacc.Bacc("TRN2", target_bir_lowering=False, num_devices=1)
    given, args = {}, {}
    for name, a in arrays.items():
        given[f"in_{name}"] = np.ascontiguousarray(a)
        args[name] = nc.dram_tensor(f"in_{name}", a.shape, mybir.dt.from_np(a.dtype), kind="ExternalInput").ap()
    out = nc.dram_tensor("out", (SEQS, SEQ, DIM), mybir.dt.float32, kind="ExternalOutput").ap()
    kept = nc.dram_tensor("kept", (P, KD, SEQS, SEQ), mybir.dt.float32, kind="Internal").ap()
    tower_kernel(nc, **args, kept=kept, out=out)
    result = run_bass_kernel_spmd(nc, [given], core_ids=[0])
    return result.results[0]["out"]
```

```python
from collections import namedtuple
from contextlib import ExitStack

import numpy as np
import concourse.bass as bass
from concourse import mybir
from concourse.alu_op_type import AluOpType as ALU

SEQS, SEQ, DIM = 8, 256, 256
HEADS, DH = 16, 64
DEPTH, WINDOW = 6, 64
INNER = HEADS * DH
HID = 682
P = 128
KD = DIM // P
TT = SEQ // P
HALF = INNER // 2
UNITS = 4
PAIRS = HEADS // 2
MT = -(-HID // P)
MLAST = HID - (MT - 1) * P
KEEP = 1.0 - 0.1
LOW = 32

CHUNKS = [(kind, t, half) for half in range(2) for kind in range(3) for t in range(TT)]
NCH = len(CHUNKS)
QK_SLOT = [c for c, (kind, _, _) in enumerate(CHUNKS) if kind < 2]

UP_BANK = (0, 1, 0, 1, 1, 1)

N_NEWTON = 11
N_LN = 3 + N_NEWTON

Stage = namedtuple("Stage", "kind seq layer")
Body = namedtuple("Body", "q a f d n_q n_a n_f n_d n_ln")


def constants():
    f32 = np.float32
    half = np.arange(0, DH, 2, dtype=f32)
    pos = np.arange(SEQ, dtype=f32)

    def tables(angle, scale_q, scale_k, gain):
        cos, sin = np.cos(angle), np.sin(angle)
        sgn = np.where(np.arange(DH) < DH // 2, -1, 1).astype(f32)
        return np.stack([cos * scale_q * gain, sin * sgn * scale_q * gain,
                         cos * scale_k, sin * sgn * scale_k], 1).astype(f32)

    dim = np.arange(DH // 2, dtype=f32)
    freq = (f32(10000.0) ** (dim / f32(DH / 2))).astype(f32)
    freq = np.concatenate([freq, freq])
    tab_g = tables((pos[:, None] / freq[None]).astype(f32), 1, 1, 1 / 8)
    inv = (1.0 / f32(10000.0) ** (half / f32(DH))).astype(f32)
    ang = (pos[:, None] * inv[None]).astype(f32)
    ang = np.concatenate([ang, ang], -1)
    base = ((half + 0.4 * DH) / (1.4 * DH)).astype(f32)
    power = ((pos - SEQ // 2) / (WINDOW // 2)).astype(f32)
    scale = (base[None] ** power[:, None]).astype(f32)
    scale = np.concatenate([scale, scale], -1)
    tab_l = tables(ang, scale, (1 / scale).astype(f32), 8)

    def tiled(t):
        return np.ascontiguousarray(t.reshape(TT, P, 4, DH).transpose(1, 0, 2, 3))

    i, j = np.arange(SEQ)[:, None], np.arange(SEQ)[None]
    neg = f32(-1e30)
    causal = np.where(j <= i, f32(0), neg)
    local = np.where((j <= i) & (i <= j + WINDOW), f32(0), neg)
    bf16 = mybir.dt.np(mybir.dt.bfloat16)
    masks = np.concatenate([causal[:P, :P], causal[P:, :], local[:P, :P], local[P:, WINDOW:]], 1)
    return {"tab_g": tiled(tab_g), "tab_l": tiled(tab_l), "masks": masks.astype(bf16),
            "eye16": np.eye(P, dtype=f32).astype(bf16), "eye32": np.eye(P, dtype=f32)}


def tower_kernel(nc, ids, emb_w, emb_u, wq, wk, wv, bqkv, wo, bo, l_wqkv, l_qk_scale, l_wo, l_par,
                 l_w1, l_w2, tab_g, tab_l, masks, eye16, eye32, kept, out):
    f32, f32r, bf16, i32 = mybir.dt.float32, mybir.dt.float32r, mybir.dt.bfloat16, mybir.dt.int32
    ACT = mybir.ActivationFunctionType
    AX = mybir.AxisListType
    ds = bass.ds

    ctx = ExitStack()
    with ctx:
        def sb(name, shape, dt=f32):
            return ctx.enter_context(nc.sbuf_tensor(name, shape, dt))

        def pb(name):
            return ctx.enter_context(nc.psum_tensor(name, [P, 512], f32))

        def sem(name):
            return ctx.enter_context(nc.semaphore(name))

        xT = sb("xT", [P, KD, SEQS, SEQ + 1])
        Wh = sb("Wh", [P, KD, 3, INNER], f32r)
        with ExitStack() as raw_weights:
            Wraw = raw_weights.enter_context(nc.sbuf_tensor("Wraw", [P, KD, 3, INNER], f32))
        Wl = sb("Wl", [P, KD, 3, INNER], f32r)
        Wo = sb("Wo", [P, PAIRS, DIM])
        with ExitStack() as before_stack:
            gu = before_stack.enter_context(nc.sbuf_tensor("gu", [P, SEQS * TT, DIM], f32))
        W1h = sb("W1h", [P, KD, 2 * HID], f32r)
        W2 = sb("W2", [P, MT, DIM])
        with ExitStack() as before_stack:
            hT = before_stack.enter_context(nc.sbuf_tensor("hT", [P, KD, SEQS, SEQ], f32))
        with ExitStack() as raw_weights:
            W1raw = raw_weights.enter_context(nc.sbuf_tensor("W1raw", [P, KD, 2 * HID], f32))
        W1l = sb("W1l", [P, KD, 2 * HID], f32r)
        G = sb("G", [P, MT, SEQ])
        tab = sb("tab", [P, TT, 4, DH])
        qks = sb("qks", [P, 2, DH])
        par = sb("par", [P, DEPTH, 18])
        bO = sb("bO", [P, KD])
        bias = sb("bias", [LOW + 6, HALF], f32r)
        pick = sb("pick", [LOW + 6, 6], f32r)
        onesN = sb("onesN", [P, P])
        idb = sb("idb", [P, P], bf16)
        idf = sb("idf", [P, P])
        mk = sb("mk", [P, P + SEQ + P + SEQ - WINDOW], bf16)
        idx = sb("idx", [P, SEQS * TT], i32)
        xsh = sb("xsh", [P, KD, SEQ], f32r)
        xsl = sb("xsl", [P, KD, SEQ], f32r)
        raw = sb("raw", [P, 2, HALF])
        sq = sb("sq", [P, 2, HALF])
        t2 = sb("t2", [P, 2, HALF])
        qr = sb("qr", [P, TT, 2, INNER])
        ssq = sb("ssq", [P, 4 * 8])
        rn = sb("rn", [P, 4 * 8])
        nt = sb("nt", [P, 4 * 8])
        V = sb("V", [P, TT, INNER])
        qTh, qTl = (sb(x, [P, 2, 2, SEQ], f32r) for x in ("qTh", "qTl"))
        kTh, kTl = (sb(x, [P, 2, 2, 2, SEQ], f32r) for x in ("kTh", "kTl"))
        Pr = sb("Pr", [P, TT, 4, SEQ])
        nm = sb("nm", [P, 2, 8])
        rs = sb("rs", [P, 2, 8])
        rr = sb("rr", [P, 2, 8])
        PT = sb("PT", [P, 4, P + SEQ])
        OT = sb("OT", [P, PAIRS, SEQ])
        xf = sb("xf", [P, KD, SEQ])
        sqF = sb("sqF", [P, KD, SEQ])
        var = sqF[:, 0, :]
        ry = sb("ry", [P, TT])
        rt = sb("rt", [P, TT])
        bG = sb("bG", [P, MT])
        xnh = sb("xnh", [P, KD, SEQ], f32r)
        xnl = sb("xnl", [P, KD, SEQ], f32r)
        gw = qr[:, :, :, :].rearrange("p a b (c d) -> p (a b c) d", d=DIM)
        emb = [V[:, e, 0:TT * DIM].rearrange("p (t c) -> p t c", c=DIM) for e in range(2)]
        cen = [xf, OT[:, 0:KD, :]]
        esum = sb("esum", [P, 2, TT])
        esq = sb("esq", [P, 2, TT])
        evar = sb("evar", [P, TT])
        hb = qr[:, :, :, :].rearrange("p a b (c d) -> p (a b c) d", d=SEQ).rearrange("p (k s) q -> p k s q", k=KD)
        bias_raw = sq[0:LOW + 6, 0, :]
        yb = [xf, V[:, 1, 0:KD * SEQ].rearrange("p (k q) -> p k q", k=KD)]
        yo = [sqF, OT[:, 0:KD, :]]

        A = [pb("A0"), pb("A1")]
        T = [pb("T0"), pb("T1")]
        S0 = pb("S0")
        S1 = ctx.enter_context(nc.psum_tensor("S1", [P, 2, 512], f32))
        O = pb("O")

        s_keep, s_hb = sem("keep"), sem("hb")
        s_const, s_ids = sem("const"), sem("ids")
        gathered = [sem("gathered0"), sem("gathered1")]
        stored = [sem("stored0"), sem("stored1")]
        w_q = [sem(f"w_q{j}") for j in range(6)]
        w_o, w_1, w_2, w_tab = sem("w_o"), sem("w_1"), sem("w_2"), sem("w_tab")
        zeroed, pad_ready = sem("zeroed"), sem("pad_ready")
        pe_e, pe_n, pe_y = sem("pe_e"), sem("pe_n"), sem("pe_y")
        pe_q, pe_tq, pe_tk = sem("pe_q"), sem("pe_tq"), sem("pe_tk")
        pe_s0, pe_s1, pe_pt, pe_o, pe_wo = (sem(x) for x in ("pe_s0", "pe_s1", "pe_pt", "pe_o", "pe_wo"))
        pe_ln, pe_w1, pe_w2 = sem("pe_ln"), sem("pe_w1"), sem("pe_w2")
        a_e, a_n, a_esq, a_y = sem("a_e"), sem("a_n"), sem("a_esq"), sem("a_y")
        a_q, a_qT, a_kT, a_x0, a_x1, a_pt, a_sq, a_gelu = (sem(x) for x in ("a_q", "a_qT", "a_kT", "a_x0", "a_x1", "a_pt", "a_sq", "a_gelu"))
        a_wh, a_w1h = sem("a_wh"), sem("a_w1h")
        v_bias = sem("v_bias")
        v_root, v_norm, v_y = sem("v_root"), sem("v_norm"), sem("v_y")
        v_qT = sem("v_qT")
        v_xs, v_kT, v_max, v_rec = sem("v_xs"), sem("v_kT"), sem("v_max"), sem("v_rec")
        v_rot, v_rn, v_ot, v_res = sem("v_rot"), sem("v_rn"), sem("v_ot"), sem("v_res")
        v_xf, v_ln, v_xn, v_hid, v_out = sem("v_xf"), sem("v_ln"), sem("v_xn"), sem("v_hid"), sem("v_out")
        v_nrm, v_tab, v_emb, v_bG = sem("v_nrm"), sem("v_tab"), sem("v_emb"), sem("v_bG")
        v_aff = sem("v_aff")
        g_wl, g_w1l = sem("g_wl"), sem("g_w1l")
        g_add, g_rot, g_p = sem("g_add"), sem("g_rot"), sem("g_p")

        block = ctx.enter_context(nc.Block())

        def least(value):
            return max(value, 0) if isinstance(value, int) else value

        def bodies(eng, body):
            def g(q, a, f):
                body(Body(Stage("G", q, 0), None if a is None else Stage("G", a, 0),
                          None if f is None else Stage("G", f, 0), None,
                          q, 0 if a is None else a, 0, 0, 0 if f is None else f))

            def l(layer, s, before="L"):
                n = SEQS * layer + s
                prev = "L" if before == "L" else "G"
                if isinstance(s, int) and s == 0:
                    a, f = Stage(prev, SEQS - 1, layer - 1), Stage(prev, SEQS - 2, layer - 1)
                elif isinstance(s, int) and s == 1:
                    a, f = Stage("L", 0, layer), Stage(prev, SEQS - 1, layer - 1)
                else:
                    a, f = Stage("L", s - 1, layer), Stage("L", s - 2, layer)
                n_f = 0 if f.kind == "G" else n - 2
                if f.kind == "G" or (isinstance(n, int) and n == 2):
                    d, n_d = None, 0
                elif isinstance(s, int) and s < 3:
                    d, n_d = Stage("L", SEQS - 3 + s, layer - 1), n - 3
                else:
                    d, n_d = Stage("L", s - 3, layer), n - 3
                body(Body(Stage("L", s, layer), a, f, d, SEQS + n, SEQS + n - 1, n_f, n_d, SEQS + n - 2))

            g(0, None, None)
            g(1, 0, None)
            g(2, 1, 0)
            with eng.Fori(3, SEQS) as s:
                g(s, s - 1, s - 2)
            l(0, 0, "G")
            l(0, 1, "G")
            l(0, 2)
            with eng.Fori(3, SEQS) as s:
                l(0, s)
            with eng.Fori(1, DEPTH) as layer:
                l(layer, 0)
                l(layer, 1)
                l(layer, 2)
                with eng.Fori(3, SEQS) as s:
                    l(layer, s)
            n = SEQS * DEPTH

            def last(seq):
                return Stage("L", seq, DEPTH - 1)
            body(Body(None, last(SEQS - 1), last(SEQS - 2), last(SEQS - 3),
                      SEQS + n, SEQS + n - 1, n - 2, n - 3, SEQS + n - 2))
            body(Body(None, None, last(SEQS - 1), last(SEQS - 2), SEQS + n, SEQS + n, n - 1, n - 2, SEQS + n - 1))
            body(Body(None, None, None, last(SEQS - 1), SEQS + n, SEQS + n, n, n - 1, SEQS + n))

        def pairs(eng, step):
            for e in range(2):
                step(0, e)
            with eng.Fori(1, SEQS // 2) as i:
                for e in range(2):
                    step(i, e)

        @block.sync
        def _(sp):
            sp.dma_start(idx[:, :], ids).then_inc(s_ids, 16)
            consts = [(tab, tab_g), (idb, eye16), (idf, eye32), (mk, masks), (par, l_par), (bO, bo)]
            for row in (0, LOW):
                sp.dma_start(bias_raw[row:row + 6, :], bqkv).then_inc(s_const, 16)
            for dst, src in consts:
                sp.dma_start(dst[:], src).then_inc(s_const, 16)

            def load_wo(src):
                sp.dma_start(Wo[:, :, :], src.rearrange("(a p) m -> p a m", p=P)).then_inc(w_o, 16)

            def load_w1(layer):
                sp.dma_start(W1raw[:, :, :], l_w1[layer].rearrange("(k p) n -> p k n", p=P)).then_inc(w_1, 16)

            def load_w2(layer):
                w2 = l_w2[layer]
                sp.dma_start(W2[:, 0:MT - 1, :], w2[0:(MT - 1) * P, :].rearrange("(m p) n -> p m n", p=P)).then_inc(w_2, 16)
                sp.dma_start(W2[0:MLAST, MT - 1, :], w2[(MT - 1) * P:HID, :]).then_inc(w_2, 16)

            def load_qkv(layer):
                for half in range(2):
                    for kind in range(3):
                        last = max(c for c, (k_, _, h_) in enumerate(CHUNKS) if (k_, h_) == (kind, half))
                        sp.wait_ge(pe_q, least(NCH * (SEQS * (layer + 1) - 1) + last + 1))
                        at = kind * INNER + half * HALF
                        for k in range(KD):
                            sp.dma_start(Wraw[:, k, kind, half * HALF:(half + 1) * HALF],
                                         l_wqkv[layer, k * P:(k + 1) * P, at:at + HALF]).then_inc(w_q[3 * half + kind], 16)

            def load_tables(layer):
                sp.wait_ge(v_rot, 8 * SEQS * (layer + 1))
                sp.dma_start(tab[:, :, :, :], tab_l).then_inc(w_tab, 16)
                sp.dma_start(qks[:].rearrange("p k d -> p (k d)"), l_qk_scale[layer].to_broadcast((P, 2 * DH))).then_inc(w_tab, 16)

            def keep(s):
                sp.wait_ge(v_res, s + 1)
                sp.dma_start(kept[:, :, s:s + 1, :], hT[:, :, s:s + 1, :]).then_inc(s_keep, 16)

            for half in range(2):
                for kind, src in enumerate((wq, wk, wv)):
                    for k in range(KD):
                        sp.dma_start(Wraw[:, k, kind, half * HALF:(half + 1) * HALF].rearrange("p (h d) -> p h d", d=DH),
                                     src[half * 8:half * 8 + 8, k * P:(k + 1) * P, :].rearrange("h p d -> p h d")
                                     ).then_inc(w_q[3 * half + kind], 16)
            load_wo(wo)
            sp.wait_ge(v_emb, 4 * SEQS)
            load_w2(0)
            for s in range(SEQS - 2):
                keep(s)
            load_qkv(0)
            load_tables(0)
            keep(SEQS - 2)
            keep(SEQS - 1)
            sp.wait_ge(pe_wo, SEQS)
            load_wo(l_wo[0])
            sp.wait_ge(v_xf, SEQS)
            sp.wait_ge(s_keep, 16 * SEQS)
            load_w1(0)
            with sp.Fori(1, DEPTH) as layer:
                load_qkv(layer)
                load_tables(layer)
                sp.wait_ge(pe_wo, SEQS * (layer + 1))
                load_wo(l_wo[layer])
                sp.wait_ge(pe_w1, 6 * SEQS * layer)
                load_w1(layer)
                sp.wait_ge(pe_w2, SEQS * layer)
                load_w2(layer)
            sp.wait_ge(pe_tk, UNITS * SEQS * (DEPTH + 1))
            sp.dma_start(hb[:, :, :, :], kept).then_inc(s_hb, 16)
            def store(i, e):
                s = 2 * i + e
                sp.wait_ge(a_y, s + 1)
                sp.dma_start(out[s].rearrange("(t p) c -> p t c", p=P), yo[e][:, :, :]).then_inc(stored[e], 16)
            pairs(sp, store)
            sp.wait_ge(stored[0], 8 * SEQS)
            sp.wait_ge(stored[1], 8 * SEQS)

        N_CONST = 16 * 8

        @block.tensor
        def _(pe):
            mm = nc.tensor.matmul
            held = {}

            def take(bank, *read):
                for s, value in held[bank.name]:
                    pe.wait_ge(s, value)
                held[bank.name] = [read]
                return bank

            def project(b, c):
                kind, t, half = CHUNKS[c]
                ps = take(A[c % 2], a_q, NCH * b.n_q + c + 1)
                if c == 0:
                    pe.wait_ge(v_xs, 2 * (b.n_q + 1))
                layer = 0 if b.q.kind == "G" else b.q.layer + 1
                if t == 0:
                    pe.wait_ge(g_wl, 6 * layer + 3 * half + kind + 1)
                cols = slice(half * HALF, (half + 1) * HALF)
                toks = slice(t * P, (t + 1) * P)
                if b.q.kind == "G":
                    j = 2 * kind + half
                    mm(ps[:, :], pick[:, j:j + 1].to_broadcast((LOW + 6, P)), bias[:, :], start=True, stop=False)
                for k in range(KD):
                    mm(ps[:, :], xsh[:, k, toks], Wh[:, k, kind, cols], start=(k == 0 and b.q.kind == "L"), stop=False)
                    mm(ps[:, :], xsh[:, k, toks], Wl[:, k, kind, cols], start=False, stop=False)
                    last = mm(ps[:, :], xsl[:, k, toks], Wh[:, k, kind, cols], start=False, stop=(k == KD - 1))
                last.then_inc(pe_q, 1)

            def turn_qk(b, u):
                half = u // 2
                n_before = b.n_a + 1
                n = UNITS * b.n_a + u + 1
                if u % 2 == 0 and b.a.kind == "G":
                    pe.wait_ge(g_add, least(8 * n_before - (4 if half == 0 else 0)))
                elif u % 2 == 0:
                    pe.wait_ge(g_rot, least(8 * (n_before - SEQS) - (4 if half == 0 else 0)))
                for kind, done, read in ((0, pe_tq, v_qT), (1, pe_tk, v_kT)):
                    ps = take(T[kind], read, n)
                    for a in range(2):
                        pair = 2 * u + a
                        for t in range(TT):
                            last = nc.tensor.transpose(ps[:, a * SEQ + t * P:a * SEQ + (t + 1) * P],
                                                       qr[:, t, kind, pair * P:(pair + 1) * P], idf[:, :])
                    last.then_inc(done, 1)

            def scores(b, u):
                n = UNITS * b.n_a + u
                causal = b.a.kind == "G"
                m0 = 0 if causal else P + SEQ
                w1 = SEQ if causal else SEQ - WINDOW
                pe.wait_ge(v_qT, n + 1)
                pe.wait_ge(v_kT, n + 1)
                pe.wait_ge(a_x0, n)
                mm(S0[:, :], idb[:, :], mk[:, None, m0:m0 + P].to_broadcast((P, 4, P)), start=True, stop=False)
                parts = ((qTh, kTh), (qTh, kTl), (qTl, kTh))
                for a in range(2):
                    for x, y in parts:
                        last = mm(S0[:, a * SEQ:(a + 1) * SEQ], x[:, u % 2, a, 0:P], y[:, u % 2, a, :, 0:P],
                                  start=False, stop=(a == 1 and x is qTl))
                last.then_inc(pe_s0, 1)
                pe.wait_ge(a_x1, n)
                for a in range(2):
                    mm(S1[:, a, 0:2 * w1], idb[:, :], mk[:, None, m0 + P:m0 + P + w1].to_broadcast((P, 2, w1)),
                       start=True, stop=False)
                    for x, y in parts:
                        last = mm(S1[:, a, 0:2 * w1], x[:, u % 2, a, P:SEQ], y[:, u % 2, a, :, SEQ - w1:SEQ],
                                  start=False, stop=(x is qTl))
                last.then_inc(pe_s1, 1)

            def turn_p(b, u, pair):
                rows = P if b.a.kind == "G" else WINDOW
                for h in (2 * pair, 2 * pair + 1):
                    pe.wait_ge(g_p, 16 * b.n_a + 4 * u + h + 1)
                    ps = take(T[h % 2], a_pt, 16 * b.n_a + 4 * u + h + 1)
                    nc.tensor.transpose(ps[:, 0:P], Pr[:, 1, h, P:SEQ], idf[:, :])
                    nc.tensor.transpose(ps[:, P:2 * P], Pr[:, 0, h, 0:P], idf[:, :])
                    nc.tensor.transpose(ps[:, 2 * P:2 * P + rows], Pr[0:rows, 1, h, 0:P], idf[0:rows, 0:rows]
                                        ).then_inc(pe_pt, 1)

            def values(b, u):
                pe.wait_ge(v_ot, UNITS * b.n_a + u)
                if u == 0 and b.f:
                    pe.wait_ge(v_ln, N_LN * (b.n_ln + 1))
                for h in range(4):
                    a, e = h // 2, h % 2
                    cols = slice((4 * u + h) * DH, (4 * u + h + 1) * DH)
                    pe.wait_ge(a_pt, 16 * b.n_a + 4 * u + h + 1)
                    mm(O[e * DH:(e + 1) * DH, a * SEQ:(a + 1) * SEQ], V[:, 0, cols], PT[:, h, P:P + SEQ],
                       start=True, stop=False)
                    last = mm(O[e * DH:(e + 1) * DH, a * SEQ + P:(a + 1) * SEQ], V[:, 1, cols], PT[:, h, 0:P],
                              start=False, stop=True)
                last.then_inc(pe_o, 1)

            def out_project(b):
                layer = 0 if b.a.kind == "G" else b.a.layer + 1
                ps = take(A[0], v_res, b.n_a + 1)
                pe.wait_ge(w_o, 16 * (layer + 1))
                pe.wait_ge(v_ot, UNITS * (b.n_a + 1))
                for m in range(KD):
                    for a in range(PAIRS):
                        last = mm(ps[:, m * SEQ:(m + 1) * SEQ], Wo[:, a, m * P:(m + 1) * P], OT[:, a, :],
                                  start=(a == 0), stop=(a == PAIRS - 1))
                last.then_inc(pe_wo, 1)

            def ln_mean(b, ready):
                ps = take(A[0], v_ln, N_LN * b.n_ln + 1)
                pe.wait_ge(*ready)
                for k in range(KD):
                    last = mm(ps[:, 0:SEQ], onesN[:, :], xf[:, k, :], start=(k == 0), stop=(k == KD - 1))
                last.then_inc(pe_ln, 1)

            def ln_var(b):
                ps = take(A[1], v_ln, N_LN * b.n_ln + 2)
                pe.wait_ge(a_sq, b.n_ln + 1)
                for k in range(KD):
                    last = mm(ps[:, 0:SEQ], onesN[:, :], sqF[:, k, :], start=(k == 0), stop=(k == KD - 1))
                last.then_inc(pe_ln, 1)

            def ln_turn(b):
                pe.wait_ge(v_ot, UNITS * b.n_a)
                pe.wait_ge(v_ln, N_LN * b.n_ln + 2)
                for t in range(TT):
                    last = nc.tensor.transpose(O[:, t * P:(t + 1) * P], var[:, t * P:(t + 1) * P], idf[:, :])
                last.then_inc(pe_ln, 1)

            def ln_spread(b):
                pe.wait_ge(v_ln, N_LN * b.n_ln + 2 + N_NEWTON)
                for t in range(TT):
                    last = nc.tensor.transpose(O[:, SEQ + t * P:SEQ + (t + 1) * P], ry[:, t:t + 1].to_broadcast((P, P)),
                                               idf[:, :])
                last.then_inc(pe_ln, 1)

            def up(b, slot):
                ps = take(A[UP_BANK[slot]], *((a_gelu, 3 * b.n_f + slot + 1) if slot < 3 else (v_hid, 3 * b.n_f + slot - 2)))
                if slot == 0:
                    pe.wait_ge(g_w1l, b.f.layer + 1)
                    pe.wait_ge(v_xn, b.n_ln + 1)
                base = HID if slot < 3 else 0
                for m in (2 * (slot % 3), 2 * (slot % 3) + 1):
                    n = P if m < MT - 1 else MLAST
                    to, cols = ps[0:n, (m % 2) * SEQ:(m % 2 + 1) * SEQ], slice(base + m * P, base + m * P + n)
                    for k in range(KD):
                        mm(to, W1h[:, k, cols], xnh[:, k, :], start=(k == 0), stop=False)
                        mm(to, W1h[:, k, cols], xnl[:, k, :], start=False, stop=False)
                        last = mm(to, W1l[:, k, cols], xnh[:, k, :], start=False, stop=(k == KD - 1))
                last.then_inc(pe_w1, 1)

            def down(b, o):
                if o == 0:
                    take(A[1], v_out, b.n_d + 1)
                    pe.wait_ge(w_2, 32 * (b.d.layer + 1))
                    pe.wait_ge(v_hid, 3 * (b.n_d + 1))
                for m in range(MT):
                    n = P if m < MT - 1 else MLAST
                    last = mm(A[1][:, o * SEQ:(o + 1) * SEQ], W2[0:n, m, o * P:(o + 1) * P], G[0:n, m, :],
                              start=(m == 0), stop=(m == MT - 1))
                if o == KD - 1:
                    last.then_inc(pe_w2, 1)

            def body(b):
                held["A1"] = [(a_q, NCH * b.n_q), (v_ln, least(N_LN * b.n_ln - (N_LN - 2)))]
                held["A0"] = held["A1"] + [(v_res, b.n_a)]
                held["T0"] = held["T1"] = [(a_pt, 16 * b.n_a)]
                ffn = b.f is not None and b.f.kind == "L"
                if b.a:
                    if b.a.kind == "L" and isinstance(b.n_a, int) and b.n_a == SEQS:
                        pe.wait_ge(pad_ready, 2)
                    turn_qk(b, 0)
                if b.d:
                    down(b, 0)
                if b.a:
                    turn_qk(b, 1)
                if b.d:
                    down(b, 1)
                if b.f:
                    ln_mean(b, (v_xf, b.n_ln + 1))
                if b.a:
                    scores(b, 0)
                if b.f:
                    ln_var(b)
                if b.q:
                    project(b, 0)
                if b.f:
                    ln_turn(b)
                if b.q:
                    project(b, 1)
                    project(b, 2)
                if b.f:
                    ln_spread(b)
                if b.a:
                    turn_p(b, 0, 0)
                if b.q:
                    project(b, 3)
                if b.a:
                    turn_p(b, 0, 1)
                    scores(b, 1)
                    values(b, 0)
                if ffn:
                    up(b, 0)
                if b.a:
                    turn_qk(b, 2)
                if ffn:
                    up(b, 1)
                if b.a:
                    turn_p(b, 1, 0)
                if ffn:
                    up(b, 2)
                if b.a:
                    turn_p(b, 1, 1)
                    scores(b, 2)
                    values(b, 1)
                if ffn:
                    up(b, 3)
                if b.q:
                    project(b, 4)
                if b.a:
                    turn_qk(b, 3)
                if b.q:
                    project(b, 5)
                    project(b, 6)
                if b.a:
                    turn_p(b, 2, 0)
                if ffn:
                    up(b, 4)
                if b.a:
                    turn_p(b, 2, 1)
                    scores(b, 3)
                    values(b, 2)
                if b.q:
                    project(b, 7)
                    project(b, 8)
                if b.a:
                    turn_p(b, 3, 0)
                if b.q:
                    project(b, 9)
                if b.a:
                    turn_p(b, 3, 1)
                if b.q:
                    project(b, 10)
                if ffn:
                    up(b, 5)
                if b.a:
                    values(b, 3)
                if b.q:
                    project(b, 11)
                if b.a:
                    out_project(b)

            pe.wait_ge(s_const, N_CONST)
            pe.wait_ge(zeroed, 8)
            def turn_norm(s, e):
                pe.wait_ge(v_norm, s + 1)
                pe.wait_ge(a_n, s)
                for k in range(KD):
                    for t in range(TT):
                        last = nc.tensor.transpose(T[1][:, k * SEQ + t * P:k * SEQ + (t + 1) * P],
                                                   cen[e][:, t, k * P:(k + 1) * P], idf[:, :])
                last.then_inc(pe_n, 1)

            def embed(i, e):
                s = 2 * i + e
                pe.wait_ge(v_emb, 4 * s + 2)
                pe.wait_ge(a_e, s)
                for k in range(KD):
                    for t in range(TT):
                        last = nc.tensor.transpose(T[0][:, k * SEQ + t * P:k * SEQ + (t + 1) * P],
                                                   emb[e][:, t, k * P:(k + 1) * P], idf[:, :])
                last.then_inc(pe_e, 1)
                if not (isinstance(s, int) and s == 0):
                    turn_norm(s - 1, 1 - e)
            pairs(pe, embed)
            turn_norm(SEQS - 1, 1)
            pe.wait_ge(v_bias, 2)
            pe.wait_ge(a_e, SEQS)
            pe.wait_ge(a_n, SEQS)
            bodies(pe, body)
            def restore(i, e):
                s = 2 * i + e
                pe.wait_ge(v_y, s + 1)
                pe.wait_ge(a_y, least(s - 1))
                for t in range(TT):
                    for k in range(KD):
                        last = nc.tensor.transpose(T[e][:, t * DIM + k * P:t * DIM + (k + 1) * P],
                                                   yb[e][:, k, t * P:(t + 1) * P], idf[:, :])
                last.then_inc(pe_y, 1)
            pairs(pe, restore)

        @block.scalar
        def _(act):
            f = nc.scalar.activation

            def evac_chunk(b, c):
                kind, t, half = CHUNKS[c]
                ps = A[c % 2]
                act.wait_ge(pe_q, NCH * b.n_q + c + 1)
                if kind == 2:
                    act.wait_ge(pe_o, UNITS * b.n_a + (2 * (half + 1) if b.a else 0))
                    f(V[:, t, half * HALF:(half + 1) * HALF], ps[:, :], ACT.Copy).then_inc(a_q, 1)
                    return
                slot = QK_SLOT.index(c)
                act.wait_ge(v_rot, least(8 * b.n_q + slot - 1))
                if b.q.kind == "L":
                    f(sq[:, slot % 2, :], ps[:, :], ACT.Square)
                f(raw[:, slot % 2, :], ps[:, :], ACT.Copy).then_inc(a_q, 1)

            def cut_qkv(b, half, kind):
                layer = 0 if b.q.kind == "G" else b.q.layer + 1
                cols = slice(half * HALF, (half + 1) * HALF)
                act.wait_ge(w_q[3 * half + kind], 32 * (layer + 1))
                f(Wh[:, :, kind, cols], Wraw[:, :, kind, cols], ACT.Copy).then_inc(a_wh, 1)

            def cut_w1(b):
                act.wait_ge(w_1, 16 * (b.q.layer + 1))
                f(W1h[:, :, :], W1raw[:, :, :], ACT.Copy).then_inc(a_w1h, 1)

            def evac_qk(b, u):
                n = UNITS * b.n_a + u
                act.wait_ge(pe_tq, n + 1)
                act.wait_ge(pe_s1, least(n - 1))
                f(qTh[:, u % 2, :, :], T[0][:, :].rearrange("p (a q) -> p a q", a=2), ACT.Copy).then_inc(a_qT, 1)
                act.wait_ge(pe_tk, n + 1)
                for e in range(2):
                    rows = slice(e * DH, (e + 1) * DH)
                    last = f(kTh[rows, u % 2, :, e, :], T[1][rows, :].rearrange("p (a q) -> p a q", a=2), ACT.Copy)
                last.then_inc(a_kT, 1)

            def exps(b, u, tile):
                n = UNITS * b.n_a + u
                w1 = SEQ if b.a.kind == "G" else SEQ - WINDOW
                if tile == 0:
                    act.wait_ge(pe_pt, 4 * n)
                act.wait_ge(v_max, 2 * n + tile + 1)
                for h in range(4):
                    if tile == 0:
                        to, of = Pr[:, 0, h, 0:P], S0[:, h * P:(h + 1) * P]
                    else:
                        to, of = Pr[:, 1, h, SEQ - w1:SEQ], S1[:, h // 2, (h % 2) * w1:(h % 2 + 1) * w1]
                    i = 4 * tile + h
                    last = f(to, of, ACT.Exp, bias=nm[:, u % 2, i:i + 1], accum_out=rs[:, u % 2, i:i + 1])
                last.then_inc((a_x0, a_x1)[tile], 1)

            def evac_p(b, u, pair):
                width = P + SEQ if b.a.kind == "G" else 2 * P + WINDOW
                for h in (2 * pair, 2 * pair + 1):
                    act.wait_ge(pe_pt, 16 * b.n_a + 4 * u + h + 1)
                    act.wait_ge(pe_o, UNITS * b.n_a + u)
                    f(PT[:, h, 0:width], T[h % 2][:, 0:width], ACT.Copy).then_inc(a_pt, 1)

            def squares(b):
                act.wait_ge(v_ln, N_LN * b.n_ln + 1)
                act.wait_ge(pe_ln, 4 * b.n_ln)
                f(sqF[:, :, :], xf[:, :, :], ACT.Square).then_inc(a_sq, 1)

            def gelus(b, slot):
                act.wait_ge(pe_w1, 6 * b.n_f + slot + 1)
                act.wait_ge(pe_w2, b.n_f)
                act.wait_ge(v_bG, b.n_f + 1)
                for m in (2 * slot, 2 * slot + 1):
                    n = P if m < MT - 1 else MLAST
                    last = f(G[0:n, m, :], A[UP_BANK[slot]][0:n, (m % 2) * SEQ:(m % 2 + 1) * SEQ], ACT.Gelu,
                             bias=bG[0:n, m:m + 1])
                last.then_inc(a_gelu, 1)

            def body(b):
                ffn = b.f is not None and b.f.kind == "L"
                first = b.q is not None and isinstance(b.q.seq, int) and b.q.seq == 0
                second = b.q is not None and b.q.kind == "L" and isinstance(b.q.seq, int) and b.q.seq == 1
                if first:
                    cut_qkv(b, 0, 0)
                if b.a:
                    evac_qk(b, 0)
                if first:
                    cut_qkv(b, 0, 1)
                    cut_qkv(b, 0, 2)
                if b.a:
                    evac_qk(b, 1)
                if b.f:
                    squares(b)
                if b.a:
                    exps(b, 0, 0)
                    exps(b, 0, 1)
                if b.q:
                    evac_chunk(b, 0)
                if first:
                    cut_qkv(b, 1, 0)
                if b.q:
                    evac_chunk(b, 1)
                if first:
                    cut_qkv(b, 1, 1)
                if b.a:
                    evac_p(b, 0, 0)
                    evac_p(b, 0, 1)
                if b.q:
                    evac_chunk(b, 2)
                if first:
                    cut_qkv(b, 1, 2)
                if b.a:
                    exps(b, 1, 0)
                    exps(b, 1, 1)
                if b.q:
                    evac_chunk(b, 3)
                if b.a:
                    evac_qk(b, 2)
                if ffn:
                    gelus(b, 0)
                    gelus(b, 1)
                if b.a:
                    evac_p(b, 1, 0)
                if ffn:
                    gelus(b, 2)
                if b.a:
                    evac_p(b, 1, 1)
                    exps(b, 2, 0)
                    exps(b, 2, 1)
                if b.q:
                    evac_chunk(b, 4)
                if b.a:
                    evac_qk(b, 3)
                if b.q:
                    evac_chunk(b, 5)
                    evac_chunk(b, 6)
                if b.a:
                    evac_p(b, 2, 0)
                    evac_p(b, 2, 1)
                    exps(b, 3, 0)
                    exps(b, 3, 1)
                if b.q:
                    evac_chunk(b, 7)
                    evac_chunk(b, 8)
                if b.a:
                    evac_p(b, 3, 0)
                if b.q:
                    evac_chunk(b, 9)
                if b.a:
                    evac_p(b, 3, 1)
                if b.q:
                    evac_chunk(b, 10)
                    evac_chunk(b, 11)
                if second:
                    cut_w1(b)

            act.wait_ge(s_const, N_CONST)
            def keep_norm(s):
                f(xT[:, :, s:s + 1, 1:SEQ + 1] if isinstance(s, int) else xT[:, :, ds(s, 1), 1:SEQ + 1],
                  T[1][:, :].rearrange("p (k o q) -> p k o q", k=KD, o=1), ACT.Copy).then_inc(a_n, 1)

            def embed(i, e):
                s = 2 * i + e
                act.wait_ge(pe_e, s + 1)
                act.wait_ge(pe_n, s)
                act.wait_ge(v_emb, 4 * s + 4)
                act.wait_ge(a_esq, s)
                for t in range(TT):
                    last = f(sqF[:, t, :], cen[e][:, t, :], ACT.Square, accum_out=esq[:, e, t:t + 1])
                last.then_inc(a_esq, 1)
                f(hT[:, :, ds(s, 1), :], T[0][:, :].rearrange("p (k o q) -> p k o q", k=KD, o=1), ACT.Copy).then_inc(a_e, 1)
                if not (isinstance(s, int) and s == 0):
                    keep_norm(s - 1)
            pairs(act, embed)
            act.wait_ge(pe_n, SEQS)
            keep_norm(SEQS - 1)
            bodies(act, body)
            def restore(i, e):
                act.wait_ge(pe_y, 2 * i + e + 1)
                act.wait_ge(stored[e], 16 * i)
                f(yo[e][:, :, :], T[e][:, :].rearrange("p (t c) -> p t c", t=TT), ACT.Copy).then_inc(a_y, 1)
            pairs(act, restore)

        @block.vector
        def _(dve):
            v = nc.vector
            MAGIC = float(0x5F3759DF)

            def chain(s, base):
                n = [0]

                def link(ins):
                    n[0] += 1
                    ins.then_inc(s, 1)
                    dve.wait_ge(s, base + n[0])
                return link

            def newton(x, y, t, link):
                link(v.tensor_scalar(t.bitcast(i32), x.bitcast(i32), 1, None, ALU.logical_shift_right))
                link(v.tensor_scalar(y.bitcast(i32), t.bitcast(i32), -1.0, MAGIC, ALU.mult, ALU.add))
                for i in range(3):
                    link(v.scalar_tensor_tensor(t, y, -0.5, y, ALU.mult, ALU.mult))
                    link(v.tensor_tensor(t, t, x, ALU.mult))
                    last = v.scalar_tensor_tensor(y, t, 1.5, y, ALU.add, ALU.mult)
                    if i < 2:
                        link(last)
                return last

            def copy(to, of):
                return v.tensor_scalar(to, of, 1.0, None, ALU.mult)

            def take_input(b):
                s = b.q.seq
                dve.wait_ge(pe_q, NCH * b.n_q)
                if b.q.kind == "G":
                    x = xT[:, :, ds(s, 1), 1:SEQ + 1]
                    copy(xsh[:, :, None, :], x).then_inc(v_xs, 1)
                    dve.wait_ge(v_xs, 2 * b.n_q + 1)
                    v.tensor_tensor(xsl[:, :, None, :], x, xsh[:, :, None, :].bitcast(f32), ALU.subtract).then_inc(v_xs, 1)
                    return
                if isinstance(b.q.layer, int):
                    dve.wait_ge(v_xn, s + 1)
                else:
                    dve.wait_ge(v_out, least(b.n_q - 2 * SEQS + 1))
                x = xT[:, 0, ds(s, 1), 1:SEQ + 1], xT[:, 1, ds(s, 1), 0:SEQ]
                for k in range(KD):
                    last = copy(xsh[:, k, None, :], x[k])
                last.then_inc(v_xs, 1)
                dve.wait_ge(v_xs, 2 * b.n_q + 1)
                for k in range(KD):
                    last = v.tensor_tensor(xsl[:, k, None, :], x[k], xsh[:, k, None, :].bitcast(f32), ALU.subtract)
                last.then_inc(v_xs, 1)

            def layer_tables(b):
                dve.wait_ge(w_tab, 32 * (b.q.layer + 1))
                for kind in range(2):
                    c, sn = 2 * kind, 2 * kind + 1
                    w = qks[:, None, kind, :].to_broadcast((P, TT, DH))
                    v.tensor_tensor(tab[:, :, c, :], tab[:, :, c, :], w, ALU.mult)
                    for x in range(2):
                        to, of = slice(32 * x, 32 * x + 32), slice(32 - 32 * x, 64 - 32 * x)
                        w = qks[:, None, kind, of].to_broadcast((P, TT, 32))
                        last = v.tensor_tensor(tab[:, :, sn, to], tab[:, :, sn, to], w, ALU.mult)
                last.then_inc(v_tab, 1)
                dve.wait_ge(v_tab, b.q.layer + 1)

            def gate_biases(b):
                dve.wait_ge(a_gelu, 3 * b.n_f)
                copy(bG[:, None, :], par[:, ds(b.f.layer, 1), 10:10 + MT]).then_inc(v_bG, 1)

            def copy_f(b):
                s = b.f.seq
                dve.wait_ge(pe_ln, 4 * b.n_ln)
                dve.wait_ge(a_sq, b.n_ln)
                dve.wait_ge(v_res, b.n_ln + 1)
                if b.f.kind == "G":
                    copy(xf[:, :, None, :], hT[:, :, ds(s, 1), :]).then_inc(v_xf, 1)
                else:
                    copy(xf[:, 0, None, :], xT[:, 0, ds(s, 1), 1:SEQ + 1])
                    copy(xf[:, 1, None, :], xT[:, 1, ds(s, 1), 0:SEQ]).then_inc(v_xf, 1)

            def evac_qk(b, u):
                n = UNITS * b.n_a + u
                dve.wait_ge(a_qT, n + 1)
                dve.wait_ge(pe_s1, least(n - 1))
                v.tensor_tensor(qTl[:, u % 2, :, :], T[0][:, :].rearrange("p (a q) -> p a q", a=2),
                                qTh[:, u % 2, :, :].bitcast(f32), ALU.subtract).then_inc(v_qT, 1)
                dve.wait_ge(a_kT, n + 1)
                for e in range(2):
                    rows = slice(e * DH, (e + 1) * DH)
                    last = v.tensor_tensor(kTl[rows, u % 2, :, e, :], T[1][rows, :].rearrange("p (a q) -> p a q", a=2),
                                           kTh[rows, u % 2, :, e, :].bitcast(f32), ALU.subtract)
                last.then_inc(v_kT, 1)

            def maxima(b, u, tile):
                n = UNITS * b.n_a + u
                w1 = SEQ if b.a.kind == "G" else SEQ - WINDOW
                if tile == 0:
                    dve.wait_ge(pe_s0, n + 1)
                    v.tensor_reduce(nm[:, u % 2, 0:4], S0[:, :].rearrange("p (h k) -> p h k", h=4), axis=AX.X,
                                    op=ALU.max, negate=True).then_inc(v_max, 1)
                else:
                    dve.wait_ge(pe_s1, n + 1)
                    v.tensor_reduce(nm[:, u % 2, 4:8], S1[:, :, 0:2 * w1].rearrange("p a (h k) -> p a h k", h=2),
                                    axis=AX.X, op=ALU.max, negate=True).then_inc(v_max, 1)

            def reciprocals(b, u):
                n = UNITS * b.n_a + u
                dve.wait_ge(a_x1, n + 1)
                v.reciprocal(rr[:, u % 2, :], rs[:, u % 2, :]).then_inc(v_rec, 1)

            def rotate(b, slot):
                c = QK_SLOT[slot]
                kind, t, half = CHUNKS[c]
                dve.wait_ge(a_q, NCH * b.n_q + c + 1)
                if b.q.kind == "L":
                    i = slot % 4
                    v.tensor_reduce(ssq[:, i * 8:(i + 1) * 8], sq[:, slot % 2, :].rearrange("p (h d) -> p h d", d=DH),
                                    axis=AX.X, op=ALU.add)
                dve.wait_ge(pe_tk, UNITS * b.n_a + (2 * (half + 1) if b.a else 0))
                r = raw[:, slot % 2, :]
                v.tensor_tensor(qr[:, t, kind, half * HALF:(half + 1) * HALF].rearrange("p (h d) -> p h d", d=DH),
                                r.rearrange("p (h d) -> p h d", d=DH),
                                tab[:, t, 2 * kind, :][:, None, :].to_broadcast((P, 8, DH)), ALU.mult)
                dve.wait_ge(g_add, least(8 * b.n_q + slot - 1))
                v.tensor_tensor(t2[:, slot % 2, :].rearrange("p (h x d) -> p h x d", x=2, d=32),
                                r.rearrange("p (h x d) -> p h x d", x=2, d=32)[:, :, ::-1, :],
                                tab[:, t, 2 * kind + 1, :].rearrange("p (x d) -> p x d", x=2)[:, None, :, :]
                                .to_broadcast((P, 8, 2, 32)), ALU.mult).then_inc(v_rot, 1)

            def norms(b, half):
                if b.q.kind == "G":
                    return
                n = 2 * (b.n_q - SEQS) + half
                link = chain(v_nrm, N_NEWTON * n)
                dve.wait_ge(v_rot, 8 * b.n_q + 4 * half + 4)
                dve.wait_ge(g_rot, 4 * n)
                link(v.tensor_scalar(ssq[:, :], ssq[:, :], 1e-24, None, ALU.max))
                newton(ssq[:, :], rn[:, :], nt[:, :], link).then_inc(v_rn, 1)

            def centre(b):
                n = b.n_ln
                dve.wait_ge(pe_ln, 4 * n + 1)
                v.tensor_tensor(xf[:, :, :], xf[:, :, :], A[0][:, None, 0:SEQ].to_broadcast((P, KD, SEQ)),
                                ALU.subtract).then_inc(v_ln, 1)

            def variance(b):
                dve.wait_ge(pe_ln, 4 * b.n_ln + 2)
                v.tensor_scalar(var[:, :], A[1][:, 0:SEQ], 1e-5, None, ALU.add).then_inc(v_ln, 1)

            def root(b):
                dve.wait_ge(pe_ln, 4 * b.n_ln + 3)
                newton(O[:, 0:SEQ:P], ry[:, :], rt[:, :], chain(v_ln, N_LN * b.n_ln + 2)).then_inc(v_ln, 1)

            def normalise(b):
                n = b.n_ln
                dve.wait_ge(pe_ln, 4 * n + 4)
                v.tensor_tensor(xf[:, :, :], xf[:, :, :], O[:, None, SEQ:2 * SEQ].to_broadcast((P, KD, SEQ)),
                                ALU.mult).then_inc(v_ln, 1)
                dve.wait_ge(v_ln, N_LN * (n + 1))
                if b.f.kind == "G":
                    copy(xT[:, :, ds(b.f.seq, 1), 1:SEQ + 1], xf[:, :, None, :]).then_inc(v_xn, 1)
                    return
                for k in range(KD):
                    last = v.tensor_scalar(xf[:, k, :], xf[:, k, :], par[:, ds(b.f.layer, 1), k],
                                           par[:, ds(b.f.layer, 1), 2 + k], ALU.mult, ALU.add)
                last.then_inc(v_aff, 1)
                dve.wait_ge(v_aff, 2 * b.n_f + 1)
                dve.wait_ge(pe_w1, 6 * b.n_f)
                copy(xnh[:, :, :], xf[:, :, :]).then_inc(v_aff, 1)
                dve.wait_ge(v_aff, 2 * b.n_f + 2)
                v.tensor_tensor(xnl[:, :, :], xf[:, :, :], xnh[:, :, :].bitcast(f32), ALU.subtract).then_inc(v_xn, 1)

            def evac_o(b, u):
                n = UNITS * b.n_a + u
                dve.wait_ge(pe_o, n + 1)
                dve.wait_ge(pe_wo, b.n_a)
                v.tensor_copy(OT[:, 2 * u:2 * u + 2, :], O[:, :].rearrange("p (a q) -> p a q", a=2)).then_inc(v_ot, 1)

            def hidden(b, slot):
                dve.wait_ge(pe_w1, 6 * b.n_f + slot + 1)
                dve.wait_ge(a_gelu, 3 * b.n_f + slot - 2)
                for m in (2 * (slot - 3), 2 * (slot - 3) + 1):
                    n = P if m < MT - 1 else MLAST
                    last = v.scalar_tensor_tensor(
                        G[0:n, m, :], A[UP_BANK[slot]][0:n, (m % 2) * SEQ:(m % 2 + 1) * SEQ],
                        par[0:n, ds(b.f.layer, 1), 4 + m], G[0:n, m, :], ALU.add, ALU.mult)
                last.then_inc(v_hid, 1)

            def add_attention(b):
                dve.wait_ge(pe_wo, b.n_a + 1)
                s = b.a.seq
                if b.a.kind == "G":
                    for k in range(KD):
                        h = hT[:, k, ds(s, 1), :]
                        last = v.scalar_tensor_tensor(h, A[0][:, None, k * SEQ:(k + 1) * SEQ], bO[:, k:k + 1], h,
                                                      ALU.add, ALU.add)
                else:
                    x = xT[:, :, ds(s, 1), 1:SEQ + 1]
                    last = v.tensor_tensor(x, x, A[0][:, :].rearrange("p (k o q) -> p k o q", k=KD, o=1), ALU.add)
                last.then_inc(v_res, 1)

            def add_ffn(b):
                dve.wait_ge(pe_w2, b.n_d + 1)
                for k in range(KD):
                    x = xT[:, k, ds(b.d.seq, 1), 1:SEQ + 1]
                    last = v.scalar_tensor_tensor(x, A[1][:, None, k * SEQ:(k + 1) * SEQ],
                                                  par[:, ds(b.d.layer, 1), 16 + k], x, ALU.add, ALU.add)
                last.then_inc(v_out, 1)

            def body(b):
                ffn = b.f is not None and b.f.kind == "L"
                first = b.q is not None and isinstance(b.q.seq, int) and b.q.seq == 0
                if b.a:
                    evac_qk(b, 0)
                if b.f:
                    copy_f(b)
                if b.q:
                    take_input(b)
                if b.a:
                    evac_qk(b, 1)
                if ffn:
                    gate_biases(b)
                if b.f:
                    centre(b)
                if b.d:
                    add_ffn(b)
                if b.a:
                    maxima(b, 0, 0)
                    maxima(b, 0, 1)
                if first and b.q.kind == "L":
                    layer_tables(b)
                if b.f:
                    variance(b)
                if b.a:
                    reciprocals(b, 0)
                if b.f:
                    root(b)
                if b.q:
                    rotate(b, 0)
                if b.f:
                    normalise(b)
                if b.a:
                    maxima(b, 1, 0)
                    maxima(b, 1, 1)
                if b.q:
                    rotate(b, 1)
                if b.a:
                    evac_o(b, 0)
                    reciprocals(b, 1)
                    evac_qk(b, 2)
                if b.q:
                    rotate(b, 2)
                    rotate(b, 3)
                    norms(b, 0)
                if b.a:
                    maxima(b, 2, 0)
                    maxima(b, 2, 1)
                    evac_o(b, 1)
                if ffn:
                    hidden(b, 3)
                if b.a:
                    reciprocals(b, 2)
                    evac_qk(b, 3)
                if b.q:
                    rotate(b, 4)
                if ffn:
                    hidden(b, 4)
                if b.a:
                    maxima(b, 3, 0)
                    maxima(b, 3, 1)
                    evac_o(b, 2)
                    reciprocals(b, 3)
                if b.q:
                    rotate(b, 5)
                    rotate(b, 6)
                if ffn:
                    hidden(b, 5)
                if b.a:
                    evac_o(b, 3)
                if b.q:
                    rotate(b, 7)
                    norms(b, 1)
                if b.a:
                    add_attention(b)

            v.memset(onesN[:, :], 1.0 / DIM).then_inc(zeroed, 1)
            v.memset(bias[:, :].bitcast(f32), 0.0).then_inc(zeroed, 1)
            v.memset(pick[:, :].bitcast(f32), 0.0).then_inc(zeroed, 1)
            v.memset(xT[:, :, :, 0:1], 0.0).then_inc(zeroed, 1)
            dve.wait_ge(s_const, N_CONST)
            dve.wait_ge(zeroed, 8)
            for row in (0, LOW):
                v.tensor_copy(pick[row:row + 6, :], idf[row:row + 6, row:row + 6])
                last = v.tensor_copy(bias[row:row + 6, :], bias_raw[row:row + 6, :])
            last.then_inc(v_bias, 1)
            dve.wait_ge(v_bias, 1)
            v.tensor_tensor(bias[LOW:LOW + 6, :], bias_raw[LOW:LOW + 6, :], bias[LOW:LOW + 6, :].bitcast(f32),
                            ALU.subtract).then_inc(v_bias, 1)

            def embed_centred(i, e):
                s = 2 * i + e
                u = gu[:, ds(s * TT, TT), :]
                dve.wait_ge(gathered[e], 64 * (i + 1))
                v.tensor_scalar(u, u, KEEP, float(np.float32(1) / np.float32(KEEP)), ALU.is_lt, ALU.mult).then_inc(v_emb, 1)
                dve.wait_ge(v_emb, 4 * s + 1)
                dve.wait_ge(pe_e, least(s - 1))
                v.tensor_tensor(emb[e], gw[:, ds(s * TT, TT), :], u, ALU.mult).then_inc(v_emb, 1)
                dve.wait_ge(v_emb, 4 * s + 2)
                v.tensor_reduce(esum[:, e, :], emb[e], axis=AX.X, op=ALU.add).then_inc(v_emb, 1)
                dve.wait_ge(v_emb, 4 * s + 3)
                dve.wait_ge(pe_n, least(s - 1))
                v.scalar_tensor_tensor(cen[e][:, :, :], esum[:, e, :, None].to_broadcast((P, TT, DIM)), -1.0 / DIM,
                                       emb[e], ALU.mult, ALU.add).then_inc(v_emb, 1)

            def embed_normalised(s, e):
                link = chain(v_root, (1 + N_NEWTON) * s)
                dve.wait_ge(a_esq, s + 1)
                link(v.tensor_scalar(evar[:, :], esq[:, e, :], 1.0 / DIM, 1e-5, ALU.mult, ALU.add))
                link(newton(evar[:, :], ry[:, :], rt[:, :], link))
                v.tensor_tensor(cen[e][:, :, :], cen[e][:, :, :], ry[:, :, None].to_broadcast((P, TT, DIM)),
                                ALU.mult).then_inc(v_norm, 1)

            def embed(i, e):
                embed_centred(i, e)
                if not (isinstance(i, int) and i == 0 and e == 0):
                    embed_normalised(2 * i + e - 1, 1 - e)
            pairs(dve, embed)
            embed_normalised(SEQS - 1, 1)
            dve.wait_ge(a_e, SEQS)
            dve.wait_ge(a_n, SEQS)
            bodies(dve, body)
            dve.wait_ge(v_out, SEQS * DEPTH)
            dve.wait_ge(s_hb, 16)
            def restore(i, e):
                s = 2 * i + e
                dve.wait_ge(pe_y, least(s - 1))
                v.tensor_tensor(yb[e][:, :, None, :], hb[:, :, ds(s, 1), :], xT[:, :, ds(s, 1), 1:SEQ + 1],
                                ALU.add).then_inc(v_y, 1)
            pairs(dve, restore)

        @block.gpsimd
        def _(pool):
            p = nc.gpsimd

            def scale_p(b, u):
                w1 = SEQ if b.a.kind == "G" else SEQ - WINDOW
                pool.wait_ge(v_rec, UNITS * b.n_a + u + 1)
                for h in range(4):
                    x, y = Pr[:, 0, h, 0:P], Pr[:, 1, h, SEQ - w1:SEQ]
                    if h == 0:
                        p.tensor_tensor(x, x, rr[:, u % 2, h:h + 1].to_broadcast((P, P)), ALU.mult)
                    else:
                        p.tensor_scalar(x, x, rr[:, u % 2, h:h + 1], 1.0, ALU.mult, ALU.mult)
                    p.tensor_scalar(y, y, rr[:, u % 2, 4 + h:5 + h], 1.0, ALU.mult, ALU.mult).then_inc(g_p, 1)

            def chunk(slot):
                kind, t, half = CHUNKS[QK_SLOT[slot]]
                return qr[:, t, kind, half * HALF:(half + 1) * HALF]

            def add_turned(b, slot):
                pool.wait_ge(v_rot, 8 * b.n_q + slot + 1)
                p.tensor_tensor(chunk(slot), chunk(slot), t2[:, slot % 2, :], ALU.add).then_inc(g_add, 1)

            def scale_qk(b, slots):
                if b.q.kind == "G":
                    return
                for slot in slots:
                    pool.wait_ge(v_rn, 2 * (b.n_q - SEQS) + slot // 4 + 1)
                    i = slot % 4
                    x = chunk(slot).rearrange("p (h d) -> p h d", d=DH)
                    pool.wait_ge(g_add, 8 * b.n_q + slot + 1)
                    p.tensor_tensor(x, x, rn[:, i * 8:(i + 1) * 8, None].to_broadcast((P, 8, DH)),
                                    ALU.mult).then_inc(g_rot, 1)

            def cut_qkv(b, half, kind):
                layer = 0 if b.q.kind == "G" else b.q.layer + 1
                cols = slice(half * HALF, (half + 1) * HALF)
                pool.wait_ge(a_wh, 6 * layer + 3 * half + kind + 1)
                p.tensor_tensor(Wl[:, :, kind, cols], Wraw[:, :, kind, cols], Wh[:, :, kind, cols].bitcast(f32),
                                ALU.subtract).then_inc(g_wl, 1)

            def cut_w1(b):
                pool.wait_ge(a_w1h, b.q.layer + 1)
                p.tensor_tensor(W1l[:, :, :], W1raw[:, :, :], W1h[:, :, :].bitcast(f32), ALU.subtract).then_inc(g_w1l, 1)

            def clear_padding(kind):
                if kind == "L":
                    pool.wait_ge(pe_pt, 16 * SEQS)
                    pool.wait_ge(pe_o, UNITS * SEQS)
                done = zeroed if kind == "G" else pad_ready
                p.memset(Pr[:, 1, :, 0:WINDOW], 0.0).then_inc(done, 1)
                p.memset(PT[:, :, 2 * P + WINDOW:P + SEQ], 0.0).then_inc(done, 1)

            def body(b):
                first = b.q is not None and isinstance(b.q.seq, int) and b.q.seq == 0
                second = b.q is not None and b.q.kind == "L" and isinstance(b.q.seq, int) and b.q.seq == 1
                if first:
                    cut_qkv(b, 0, 0)
                    cut_qkv(b, 0, 1)
                    cut_qkv(b, 0, 2)
                if b.a:
                    if b.a.kind == "L" and isinstance(b.n_a, int) and b.n_a == SEQS:
                        clear_padding("L")
                    scale_p(b, 0)
                if b.q:
                    add_turned(b, 0)
                    add_turned(b, 1)
                if b.a:
                    scale_p(b, 1)
                if b.q:
                    add_turned(b, 2)
                    add_turned(b, 3)
                if first:
                    cut_qkv(b, 1, 0)
                if b.q:
                    scale_qk(b, (0, 1))
                if first:
                    cut_qkv(b, 1, 1)
                if b.a:
                    scale_p(b, 2)
                if b.q:
                    scale_qk(b, (2, 3))
                    add_turned(b, 4)
                if first:
                    cut_qkv(b, 1, 2)
                if b.a:
                    scale_p(b, 3)
                if b.q:
                    add_turned(b, 5)
                    add_turned(b, 6)
                    add_turned(b, 7)
                    scale_qk(b, (4, 5, 6, 7))
                if second:
                    cut_w1(b)

            p.memset(kTh[:, :, :, :, :].bitcast(f32), 0.0).then_inc(zeroed, 1)
            p.memset(kTl[:, :, :, :, :].bitcast(f32), 0.0).then_inc(zeroed, 1)
            clear_padding("G")
            pool.wait_ge(s_ids, 16)
            for s in range(SEQS):
                pool.wait_ge(gathered[s % 2], 64 * (s // 2))
                for t in range(s * TT, (s + 1) * TT):
                    for table, to in ((emb_w, gw), (emb_u, gu)):
                        p.indirect_dma_start(out=to[:, t, :], out_offset=None, in_=table[:, :],
                                             in_offset=bass.IndirectOffsetOnAxis(ap=idx[:, t:t + 1], axis=0)
                                             ).then_inc(gathered[s % 2], 16)
            bodies(pool, body)


def kernel(**inputs):
    import concourse.bacc as bacc
    from concourse.bass_utils import run_bass_kernel_spmd

    x = {k: np.ascontiguousarray(a) for k, a in inputs.items()}

    def halves(a, width):
        return a.reshape(DEPTH, -1, width).transpose(2, 0, 1)

    def tiles(a):
        padded = np.zeros((DEPTH, MT * P), a.dtype)
        padded[:, :HID] = a
        return halves(padded, P)

    b1 = x["L0_ffn_b1"]
    params = np.concatenate([halves(x["L0_ffn_ln_g"], P), halves(x["L0_ffn_ln_b"], P), tiles(b1[:, :HID]),
                             tiles(b1[:, HID:]), halves(x["L0_ffn_b2"], P)], 2)
    arrays = {
        "ids": x["x"].reshape(SEQS * TT, P).T,
        "emb_w": x["L0_tok_weight"], "emb_u": x["L0_tok_mask_u"],
        "wq": x["L0_attn_W_Q"], "wk": x["L0_attn_W_K"], "wv": x["L0_attn_W_V"],
        "bqkv": np.concatenate([x[f"L0_attn_b_{n}"].reshape(2, HALF) for n in "QKV"]),
        "wo": x["L0_attn_W_O"].reshape(INNER, DIM), "bo": x["L0_attn_b_O"].reshape(KD, P).T,
        "l_wqkv": x["L0_ffn_Wqkv"],
        "l_qk_scale": np.stack([x["L0_ffn_q_scale"], x["L0_ffn_k_scale"]], 1).reshape(DEPTH, 1, -1),
        "l_wo": x["L0_ffn_Wo"], "l_par": params, "l_w1": x["L0_ffn_W1"], "l_w2": x["L0_ffn_W2"],
        **constants(),
    }
    nc = bacc.Bacc("TRN2", target_bir_lowering=False, num_devices=1)
    given, args = {}, {}
    for name, a in arrays.items():
        given[f"in_{name}"] = np.ascontiguousarray(a)
        args[name] = nc.dram_tensor(f"in_{name}", a.shape, mybir.dt.from_np(a.dtype), kind="ExternalInput").ap()
    out = nc.dram_tensor("out", (SEQS, SEQ, DIM), mybir.dt.float32, kind="ExternalOutput").ap()
    kept = nc.dram_tensor("kept", (P, KD, SEQS, SEQ), mybir.dt.float32, kind="Internal").ap()
    tower_kernel(nc, **args, kept=kept, out=out)
    result = run_bass_kernel_spmd(nc, [given], core_ids=[0])
    return result.results[0]["out"]
```
